# Optimizing a Trainium2 kernel written in Bass

```python
import numpy as np
import jax
import jax.numpy as jnp

def _softmax(x, axis=-1):
    return jax.nn.softmax(x, axis=axis)

def _gelu(x):
    return jax.nn.gelu(x, approximate=True)

def _silu(x):
    return jax.nn.silu(x)

def _sigmoid(x):
    return jax.nn.sigmoid(x)

def _layernorm(x, axis=-1, eps=1e-05):
    m = jnp.mean(x, axis=axis, keepdims=True)
    v = jnp.var(x, axis=axis, keepdims=True)
    return (x - m) / jnp.sqrt(v + eps)

def _scatter_add(tgt, idx, src, axis=0):
    return tgt.at[idx].add(src)

def _segment_sum(src, seg, n):
    return jax.ops.segment_sum(src, seg, n)
kernel_name = 'mk_gnn_ffn_d2_gnn_r8_ccc0ea'

def setup_inputs(seed: int=0):
    np.random.seed(seed)
    _w = jnp.asarray

    def _rec_inputs():
        import jax
        import jax.numpy as jnp
        _gk = jax.random.key(seed)
        x = 0.5 + 0.2886 * jax.random.normal(jax.random.fold_in(_gk, 1), (1250, 1024), jnp.float32)
        _s = jax.random.randint(jax.random.fold_in(_gk, 2), (10000,), 0, 1250, jnp.int32)
        _d = jax.random.randint(jax.random.fold_in(_gk, 3), (10000,), 0, 1250, jnp.int32)
        _loop = jnp.arange(1250, dtype=jnp.int32)
        src = jnp.concatenate([_s, _d, _loop])
        dst = jnp.concatenate([_d, _s, _loop])
        _o = jnp.argsort(dst, stable=True)
        src = src[_o]
        dst = dst[_o]
        edge_type_8 = jax.random.randint(jax.random.fold_in(_gk, 12), (21250,), 0, 8, jnp.int32)
        edge_weight = jax.random.uniform(jax.random.fold_in(_gk, 13), (21250,), jnp.float32, 0.0, 0.999998)
        return (x, src, dst, edge_type_8, edge_weight)
    x, src, dst, edge_type_8, edge_weight = _rec_inputs()

    def _L0_gnn_setup():
        import jax, jax.numpy as jnp
        import numpy as np
        N_NODES = 6250
        N_EDGES = 100000
        IN_SIZE = 1024
        EMB = 500
        key = jax.random.key(seed)
        ks = jax.random.split(key, 9)
        x = jax.random.uniform(ks[0], (N_NODES, IN_SIZE), dtype=jnp.float32)
        edge_index = jax.random.randint(ks[1], (2, N_EDGES), 0, N_NODES, dtype=jnp.int32)
        edge_weight = jax.random.uniform(ks[2], (N_EDGES,), dtype=jnp.float32)
        s = 0.05
        wenc = jax.random.normal(ks[3], (EMB, IN_SIZE), dtype=jnp.float32) * s
        benc = jax.random.normal(ks[4], (EMB,), dtype=jnp.float32) * s
        wdec = jax.random.normal(ks[5], (IN_SIZE, EMB), dtype=jnp.float32) * s
        bdec = jax.random.normal(ks[6], (IN_SIZE,), dtype=jnp.float32) * s
        conv_weight = jax.random.normal(ks[7], (EMB, EMB), dtype=jnp.float32) * 0.1
        lin_weight = jax.random.normal(ks[8], (EMB, EMB), dtype=jnp.float32) * 0.1 + jnp.eye(EMB, dtype=jnp.float32)
        return {'x': x, 'edge_index': edge_index, 'edge_weight': edge_weight, 'wenc': wenc, 'benc': benc, 'wdec': wdec, 'bdec': bdec, 'conv_weight': conv_weight, 'lin_weight': lin_weight}
    _L0_gnn_all = _L0_gnn_setup()
    _L0_gnn_in = {k: v for k, v in _L0_gnn_all.items() if k in ('wenc', 'benc', 'wdec', 'bdec', 'conv_weight', 'lin_weight')}
    del _L0_gnn_all

    def _L0_ffn_setup():
        import jax, jax.numpy as jnp
        import numpy as np
        B, S, D, H, E, K = (4, 256, 1024, 512, 4, 2)
        key = jax.random.key(seed)
        ks = jax.random.split(key, 7)
        s1 = 1.0 / np.sqrt(D)
        s2 = 1.0 / np.sqrt(H)
        return {'x': jax.random.normal(ks[0], (B, S, D), jnp.float32), 'w1': jax.random.uniform(ks[1], (E, D, H), jnp.float32, -s1, s1), 'b1': jax.random.uniform(ks[2], (E, H), jnp.float32, -s1, s1), 'w2': jax.random.uniform(ks[3], (E, H, D), jnp.float32, -s2, s2), 'b2': jax.random.uniform(ks[4], (E, D), jnp.float32, -s2, s2), 'wr': jax.random.uniform(ks[5], (D, E), jnp.float32, -s1, s1), 'br': jax.random.uniform(ks[6], (E,), jnp.float32, -s1, s1)}
    _L0_ffn_all = _L0_ffn_setup()
    _L0_ffn_in = {k: v for k, v in _L0_ffn_all.items() if k in ('w1', 'b1', 'w2', 'b2', 'wr', 'br')}
    del _L0_ffn_all

    def _L1_gnn_setup():
        import jax, jax.numpy as jnp
        import numpy as np
        N, D, R, E = (1250, 1024, 8, 10000)

        def _rgcn(x, edge_index, edge_type, weight, root, bias):
            src, dst = (edge_index[0], edge_index[1])
            msgs = x[src]
            out = x @ root + bias
            n = x.shape[0]
            for r in range(weight.shape[0]):
                mask = (edge_type == r).astype(x.dtype)
                sums = jax.ops.segment_sum(msgs * mask[:, None], dst, num_segments=n)
                cnt = jax.ops.segment_sum(mask, dst, num_segments=n)
                mean = sums / jnp.maximum(cnt, 1.0)[:, None]
                out = out + mean @ weight[r]
            return out
        key = jax.random.key(seed)
        ks = jax.random.split(key, 8)
        s = 1.0 / np.sqrt(D)
        x = jax.random.normal(ks[0], (N, D), dtype=jnp.float32)
        edge_index = jax.random.randint(ks[1], (2, E), 0, N, dtype=jnp.int64)
        edge_type = jax.random.randint(ks[2], (E,), 0, R, dtype=jnp.int64)
        weight = jax.random.normal(ks[3], (R, D, D), dtype=jnp.float32) * s
        root = jax.random.normal(ks[4], (D, D), dtype=jnp.float32) * s
        bias = jnp.zeros((D,), dtype=jnp.float32)
        w_gate = jax.random.normal(ks[5], (2 * D, D), dtype=jnp.float32) * (1.0 / np.sqrt(2 * D))
        b_gate = jnp.zeros((D,), dtype=jnp.float32)
        return {'x': x, 'edge_index': edge_index, 'edge_type': edge_type, 'weight': weight, 'root': root, 'bias': bias, 'w_gate': w_gate, 'b_gate': b_gate}
    _L1_gnn_all = _L1_gnn_setup()
    _L1_gnn_in = {k: v for k, v in _L1_gnn_all.items() if k in ('weight', 'root', 'bias', 'w_gate', 'b_gate')}
    del _L1_gnn_all

    def _L1_ffn_setup():
        import jax, jax.numpy as jnp
        import numpy as np
        D_MODEL = 1024
        D_FF = 512
        NUM_EXPERTS = 8
        key = jax.random.key(seed)
        ks = jax.random.split(key, 8)
        scale_in = 1.0 / np.sqrt(D_MODEL)
        scale_ff = 1.0 / np.sqrt(D_FF)
        x = jax.random.normal(ks[0], (4, 256, D_MODEL), dtype=jnp.float32)
        gate_w = jax.random.uniform(ks[1], (NUM_EXPERTS, D_MODEL), jnp.float32, -scale_in, scale_in)
        gate_b = jax.random.uniform(ks[2], (NUM_EXPERTS,), jnp.float32, -scale_in, scale_in)
        expert_bias = jnp.zeros((NUM_EXPERTS,), dtype=jnp.float32)
        w1 = jax.random.uniform(ks[3], (NUM_EXPERTS, D_MODEL, D_FF), jnp.float32, -scale_in, scale_in)
        b1 = jax.random.uniform(ks[4], (NUM_EXPERTS, D_FF), jnp.float32, -scale_in, scale_in)
        w2 = jax.random.uniform(ks[5], (NUM_EXPERTS, D_FF, D_MODEL), jnp.float32, -scale_ff, scale_ff)
        b2 = jax.random.uniform(ks[6], (NUM_EXPERTS, D_MODEL), jnp.float32, -scale_ff, scale_ff)
        return {'x': x, 'gate_w': gate_w, 'gate_b': gate_b, 'expert_bias': expert_bias, 'w1': w1, 'b1': b1, 'w2': w2, 'b2': b2}
    _L1_ffn_all = _L1_ffn_setup()
    _L1_ffn_in = {k: v for k, v in _L1_ffn_all.items() if k in ('gate_w', 'gate_b', 'expert_bias', 'w1', 'b1', 'w2', 'b2')}
    del _L1_ffn_all
    return {'x': x, 'src': src, 'dst': dst, 'edge_type_8': edge_type_8, 'edge_weight': edge_weight, 'L0_gnn_wenc': _L0_gnn_in['wenc'], 'L0_gnn_benc': _L0_gnn_in['benc'], 'L0_gnn_wdec': _L0_gnn_in['wdec'], 'L0_gnn_bdec': _L0_gnn_in['bdec'], 'L0_gnn_conv_weight': _L0_gnn_in['conv_weight'], 'L0_gnn_lin_weight': _L0_gnn_in['lin_weight'], 'L0_ffn_w1': _L0_ffn_in['w1'], 'L0_ffn_b1': _L0_ffn_in['b1'], 'L0_ffn_w2': _L0_ffn_in['w2'], 'L0_ffn_b2': _L0_ffn_in['b2'], 'L0_ffn_wr': _L0_ffn_in['wr'], 'L0_ffn_br': _L0_ffn_in['br'], 'L1_gnn_weight': _L1_gnn_in['weight'], 'L1_gnn_root': _L1_gnn_in['root'], 'L1_gnn_bias': _L1_gnn_in['bias'], 'L1_gnn_w_gate': _L1_gnn_in['w_gate'], 'L1_gnn_b_gate': _L1_gnn_in['b_gate'], 'L1_ffn_gate_w': _L1_ffn_in['gate_w'], 'L1_ffn_gate_b': _L1_ffn_in['gate_b'], 'L1_ffn_expert_bias': _L1_ffn_in['expert_bias'], 'L1_ffn_w1': _L1_ffn_in['w1'], 'L1_ffn_b1': _L1_ffn_in['b1'], 'L1_ffn_w2': _L1_ffn_in['w2'], 'L1_ffn_b2': _L1_ffn_in['b2']}

def reference(x, src, dst, edge_type_8, edge_weight, L0_gnn_wenc, L0_gnn_benc, L0_gnn_wdec, L0_gnn_bdec, L0_gnn_conv_weight, L0_gnn_lin_weight, L0_ffn_w1, L0_ffn_b1, L0_ffn_w2, L0_ffn_b2, L0_ffn_wr, L0_ffn_br, L1_gnn_weight, L1_gnn_root, L1_gnn_bias, L1_gnn_w_gate, L1_gnn_b_gate, L1_ffn_gate_w, L1_ffn_gate_b, L1_ffn_expert_bias, L1_ffn_w1, L1_ffn_b1, L1_ffn_w2, L1_ffn_b2):
    import jax
    import jax.numpy as jnp

    def _L0_gnn_ref(x, edge_index, edge_weight, wenc, benc, wdec, bdec, conv_weight, lin_weight):
        import jax, jax.numpy as jnp
        import numpy as np
        N_NODES = 6250
        N_EDGES = 100000
        IN_SIZE = 1024
        EMB = 500
        h = jax.nn.sigmoid(x @ wenc.T + benc)
        h2 = h @ conv_weight
        src, dst = (edge_index[0], edge_index[1])
        msgs = h2[src] * edge_weight[:, None]
        agg = jax.ops.segment_sum(msgs, dst, num_segments=x.shape[0])
        hout = agg + h @ lin_weight.T
        p = hout @ wdec.T + bdec
        return p

    def _L0_ffn_ref(x, w1, b1, w2, b2, wr, br):
        import jax, jax.numpy as jnp
        import numpy as np
        B, S, D, H, E, K = (4, 256, 1024, 512, 4, 2)
        Bx, Sx, Dx = x.shape
        xf = x.reshape(-1, Dx)
        logits = xf @ wr + br
        topk_vals, topk_idx = jax.lax.top_k(logits, K)
        gates = jax.nn.softmax(topk_vals, axis=-1)
        h = jax.nn.gelu(jnp.einsum('nd,edh->enh', xf, w1) + b1[:, None, :], approximate=False)
        y = jnp.einsum('enh,ehd->end', h, w2) + b2[:, None, :]
        c = jnp.einsum('eh,ehd->ed', jax.nn.gelu(b1, approximate=False), w2) + b2
        c_sum = c.sum(axis=0)
        yt = jnp.transpose(y, (1, 0, 2))
        y_sel = jnp.take_along_axis(yt, topk_idx[:, :, None], axis=1)
        c_sel = c[topk_idx]
        out = jnp.einsum('nk,nkd->nd', gates, y_sel - c_sel + c_sum[None, None, :])
        return out.reshape(Bx, Sx, Dx)

    def _L1_gnn_ref(x, edge_index, edge_type, weight, root, bias, w_gate, b_gate):
        import jax, jax.numpy as jnp
        import numpy as np
        N, D, R, E = (1250, 1024, 8, 10000)

        def _rgcn(x, edge_index, edge_type, weight, root, bias):
            src, dst = (edge_index[0], edge_index[1])
            msgs = x[src]
            out = x @ root + bias
            n = x.shape[0]
            for r in range(weight.shape[0]):
                mask = (edge_type == r).astype(x.dtype)
                sums = jax.ops.segment_sum(msgs * mask[:, None], dst, num_segments=n)
                cnt = jax.ops.segment_sum(mask, dst, num_segments=n)
                mean = sums / jnp.maximum(cnt, 1.0)[:, None]
                out = out + mean @ weight[r]
            return out
        u = _rgcn(x, edge_index, edge_type, weight, root, bias)
        z = jnp.concatenate([u, x], axis=1) @ w_gate + b_gate
        h = jnp.tanh(u) * z + x * (1.0 - z)
        return h

    def _L1_ffn_ref(x, gate_w, gate_b, expert_bias, w1, b1, w2, b2):
        import jax, jax.numpy as jnp
        import numpy as np
        D_MODEL = 1024
        D_FF = 512
        NUM_EXPERTS = 8
        gate_logits = jnp.einsum('bsd,ed->bse', x, gate_w) + gate_b + expert_bias
        top_idx = jnp.argmax(gate_logits, axis=-1)
        out = jnp.zeros_like(x)
        for e in range(NUM_EXPERTS):
            mask = (top_idx == e)[..., None].astype(x.dtype)
            h = jax.nn.relu(jnp.einsum('bsd,df->bsf', x, w1[e]) + b1[e])
            y = jnp.einsum('bsf,fd->bsd', h, w2[e]) + b2[e]
            out = out + mask * y
        return out
    edge_index = jnp.stack([src, dst])
    x = x + _L0_gnn_ref(_layernorm(x, axis=-1), edge_index, edge_weight, L0_gnn_wenc, L0_gnn_benc, L0_gnn_wdec, L0_gnn_bdec, L0_gnn_conv_weight, L0_gnn_lin_weight)
    x = x + _L0_ffn_ref(_layernorm(x, axis=-1)[None], L0_ffn_w1, L0_ffn_b1, L0_ffn_w2, L0_ffn_b2, L0_ffn_wr, L0_ffn_br)[0]
    x = x + _L1_gnn_ref(_layernorm(x, axis=-1), edge_index, edge_type_8, L1_gnn_weight, L1_gnn_root, L1_gnn_bias, L1_gnn_w_gate, L1_gnn_b_gate)
    x = x + _L1_ffn_ref(_layernorm(x, axis=-1)[None], L1_ffn_gate_w, L1_ffn_gate_b, L1_ffn_expert_bias, L1_ffn_w1, L1_ffn_b1, L1_ffn_w2, L1_ffn_b2)[0]
    return x

_drawn_inputs = setup_inputs


def setup_inputs(seed=0):
    import zlib

    import numpy as np

    out = dict(_drawn_inputs(seed))
    spreads = {'L1_gnn_bias': (0.0, 0.694),
     'L1_gnn_b_gate': (0.0, 0.745),
     'L1_ffn_expert_bias': (0.0, 0.616)}
    factors = {'L0_gnn_benc': 3.094,
     'L0_gnn_bdec': 8.0,
     'L0_ffn_w1': 4.139,
     'L0_ffn_b1': 8.0,
     'L0_ffn_w2': 3.948,
     'L0_ffn_b2': 8.0,
     'L0_ffn_wr': 5.093,
     'L0_ffn_br': 22.935,
     'L1_ffn_gate_w': 3.125,
     'L1_ffn_gate_b': 8.0,
     'L1_ffn_w1': 3.697,
     'L1_ffn_b1': 34.825,
     'L1_ffn_w2': 3.104,
     'L1_ffn_b2': 30.443}
    for name, (base, spread) in spreads.items():
        noise = np.random.default_rng([zlib.crc32(name.encode()), seed]).standard_normal(out[name].shape)
        drawn = base * np.exp(spread * noise) if base else spread * noise
        out[name] = jnp.asarray(drawn.astype(out[name].dtype))
    for name, factor in factors.items():
        out[name] = (out[name] * factor).astype(out[name].dtype)
    return out
```

```python
from contextlib import ExitStack

import concourse.bass as bass
import numpy as np
from concourse import mybir

F32 = mybir.dt.float32
BF16 = mybir.dt.bfloat16
I32 = mybir.dt.int32
U32 = mybir.dt.uint32
ALU = mybir.AluOpType
ACT = mybir.ActivationFunctionType
AX = mybir.AxisListType

P = 128
N_NODES = 1250
D = 1024
NT = -(-N_NODES // P)
NPAD = NT * P
LAST = N_NODES - (NT - 1) * P
KD = D // P
HALF = 512
EMB = 500
EMBP = 512
EMBC = EMBP - 8
KE = EMBP // P
N_EDGES = 21250
ET = -(-N_EDGES // P)
RING = 8
BATCH = 4
SLOTS = -(-((N_EDGES + NT * (P - 1)) // P) // RING) * RING
REL = 8
E0 = 4
HID = 512
KH = HID // P
E1 = 8
TSLOTS = -(-((N_NODES + E1 * (P - 1)) // P) // 2) * 2
EPS = 1e-5
RELBITS = 3
ROWSHIFT = 14
NOWHERE = 1.0e6
TOKG = [(0, 512), (512, 512), (1024, 256)]
SUMROW = LAST

UNIT_ENC, UNIT_CONVLIN, UNIT_DEC, UNIT_E0 = 0, 1, 2, 3
UNIT_REL = UNIT_E0 + 2 * E0
UNIT_ROOT = UNIT_REL + 2 * REL
UNIT_GATE = UNIT_ROOT + 2
UNIT_E1 = UNIT_GATE + 4

T_LN1 = 0
T_AGG = T_LN1 + 2 * NT
T_LN2 = T_AGG + NT
T_LN3 = T_LN2 + 2 * NT
T_U = T_LN3 + 2 * NT
T_LN4 = T_U + 4 * NT
T_SLOT = T_LN4 + 2 * NT
A_ENC = 0
A_H2 = A_ENC + KE * len(TOKG)
A_LIN = A_H2 + NT
A_UP = A_LIN + NT
A_Y = A_UP + E0 * KH * len(TOKG)
V_PRE = 0

V_DEC = 1
V_ROUTE = V_DEC + 2 * NT
V_DOWN = V_ROUTE + 1
V_CSUM = V_DOWN + E0 * 2 * NT
V_ROOT = V_CSUM + 2
V_GATE = V_ROOT + 2 * NT
V_ROUTE2 = V_GATE + 2 * NT
V_PRE2 = V_ROUTE2 + 1
V_LIST2 = V_PRE2 + 1
V_SLOT = V_LIST2 + 1


def build(nc, a, out):
    ctx = ExitStack()
    with ctx:
        def sb(name, shape, dt=F32):
            return ctx.enter_context(nc.sbuf_tensor(name, shape, dt))

        def sem(name):
            return ctx.enter_context(nc.semaphore(name))

        def dram(name, shape):
            return nc.dram_tensor(name, shape, F32, kind="Internal").ap()

        h2_dram = dram("h2_rows", (NPAD, EMBP))
        y_dram = dram("y_rows", (NPAD, REL, D))
        inv_dram = dram("inv_count", (NPAD, REL))
        xn_dram = dram("xn_rows", (NPAD, D))
        moe_dram = dram("moe_rows", (TSLOTS * P, D))

        X = sb("X", [P, NT, D])
        XT = sb("XT", [P, KD, NPAD])
        W = sb("W", [P, 2, 8 * HALF])
        U = sb("U", [P, NT * D])
        room = sb("room", [P, 4, D])
        rows_h2 = room[:].rearrange("p b (c n) -> p (b c) n", n=EMBP)
        rows_y = W[:].rearrange("p b (c n) -> p (b c) n", n=D)
        XN = sb("XN", [P, 2, D])
        OS = sb("OS", [P, 4, HALF])
        u_rows = U[:].rearrange("p (m n) -> p m n", m=NT)
        hT = U[:, 0:KE * NPAD].rearrange("p (c n) -> p c n", c=KE)
        agg = U[:, KE * NPAD:].rearrange("p (m n) -> p m n", m=NT)
        lane = U[:, KE * NPAD:]
        used = [0]

        def scratch(n):
            used[0] += n
            assert used[0] <= KE * NPAD
            return lane[:, used[0] - n:used[0]]

        e_dst = scratch(ET).bitcast(I32)
        e_src = scratch(ET).bitcast(I32)
        e_typ = scratch(ET).bitcast(I32)
        e_w = scratch(ET)
        e_t0 = scratch(ET).bitcast(I32)
        e_t1 = scratch(ET).bitcast(I32)
        e_key = scratch(ET)
        e_hot = scratch(NT * ET)
        e_cum = scratch(NT * ET)
        e_pos = scratch(ET)
        e_lane = scratch(ET)
        e_slot = scratch(ET)
        e_pack = e_key
        perm_lane = room[:, :, 0:P]
        perm_val = room[:, :, P:P + 2 * SLOTS]

        iota_free = sb("iota_free", [P, SLOTS])
        iota_part = sb("iota_part", [P, 1])
        ident = sb("ident", [P, P])
        before = sb("before", [P, P])
        ones = sb("ones", [P, P])
        sel_sum = sb("sel_sum", [P, P])
        pad_mask = sb("pad_mask", [P, 3])
        eps = sb("eps", [P, 1])

        l_pack = sb("l_pack", [P, SLOTS], I32)
        l_w = sb("l_w", [P, SLOTS])
        l_src = sb("l_src", [P, SLOTS], I32)
        l_row8 = sb("l_row8", [P, SLOTS], I32)
        l_rel = sb("l_rel", [P, SLOTS])
        l_row = sb("l_row", [P, SLOTS])
        l_tile = sb("l_tile", [P, SLOTS], I32)
        l_inv_at = sb("l_inv_at", [P, SLOTS], I32)
        l_inv = sb("l_inv", [P, SLOTS])
        l_tmp = sb("l_tmp", [P, SLOTS])
        at_ring = sb("at_ring", [P, 2, RING], I32)
        inv_ring = sb("inv_ring", [P, RING])
        hot = XN[:, 0, :].rearrange("p (c n) -> p c n", n=P)
        hot1 = sb("hot1", [P, RING, P], BF16)
        hotr = sb("hotr", [P, RING, REL], BF16)
        count = sb("count", [P, NT, REL])

        pre = sb("pre", [P, 8, NT])
        prei = sb("prei", [P, 2, NT], I32)
        stats = sb("stats", [P, 2, 2, 6])
        mv = sb("mv", [P, NT, 2])
        std = sb("std", [P, NT])
        rstd = sb("rstd", [P, NT])

        b_enc = sb("b_enc", [P, KE])
        b_up = sb("b_up", [P, E0 * KH])
        g_up = sb("g_up", [P, E0 * KH])
        b2_rows = sb("b2_rows", [E0, D])
        w_route = sb("w_route", [P, KD, E0])
        b_route = sb("b_route", [P, E0])
        w_route2 = sb("w_route2", [P, KD, E1])
        b_route2 = sb("b_route2", [P, 2, E1])
        logits = sb("logits", [P, NT, 8])
        top = sb("top", [P, NT, 8])
        top_at = sb("top_at", [P, NT, 8], U32)
        top_f = sb("top_f", [P, NT, 8])
        gsm = sb("gsm", [P, 6, NT])
        gates = sb("gates", [P, NT, E0])
        tok_hot = sb("tok_hot", [P, E1 * NT])
        tok_cum = sb("tok_cum", [P, E1 * NT])
        tok_key = sb("tok_key", [P, NT])
        tok_id = sb("tok_id", [P, NT])
        tok_pad = sb("tok_pad", [P, NT])
        tok_pos = sb("tok_pos", [P, NT])
        tok_posi = sb("tok_posi", [P, NT], I32)
        tok_t = sb("tok_t", [P, 2, NT], I32)
        tok_lane = sb("tok_lane", [P, NT])
        tok_slot = sb("tok_slot", [P, NT])
        tok_list = sb("tok_list", [P, TSLOTS], I32)
        slot_exp = sb("slot_exp", [P, TSLOTS], I32)
        slot_tmp = sb("slot_tmp", [P, TSLOTS])

        b_dec = room[:, 0, :]
        b_rgcn = XN[:, 1, :]
        b_gate = OS[:, 2:4, :].rearrange("p c n -> p (c n)")
        uT = room[:, 0:2, :].rearrange("p b (k n) -> p b k n", k=KD)
        mixed = room[:, 2:4, 0:HALF]
        xn_half = room[:, 2:4, HALF:D]
        tok_perm_lane = room[:, 0:2, :].rearrange("p b (c n) -> p (b c) n", n=P)
        tok_perm_val = room[:, 2, 0:NT * TSLOTS].rearrange("p (t s) -> p t s", t=NT)
        tok_rows = U[:, 0:2 * D].rearrange("p (b n) -> p b n", b=2)
        tok_xT = U[:, 2 * D:4 * D].rearrange("p (b k n) -> p b k n", b=2, k=KD)
        tok_h = U[:, 4 * D:5 * D].rearrange("p (b n) -> p b n", b=2)
        tok_hT = U[:, 5 * D:6 * D].rearrange("p (b k n) -> p b k n", b=2, k=KH)
        tok_b1 = U[:, 6 * D:7 * D].rearrange("p (b n) -> p b n", b=2)
        tok_b2 = U[:, 7 * D:9 * D].rearrange("p (b n) -> p b n", b=2)
        moe_rows = XT[:].rearrange("p k n -> p (k n)").rearrange("p (m n) -> p m n", m=NT)

        pairs = [ctx.enter_context(nc.psum_tensor(f"pair{i}", [P, D], F32)) for i in range(4)]
        banks = [pairs[i // 2][:, (i % 2) * HALF:(i % 2 + 1) * HALF] for i in range(8)]
        a_bank, v_bank, t_bank = banks[0:2], banks[2:4], banks[4:6]
        sum_bank = [banks[2], banks[3], banks[6], banks[7]]
        list_bank = banks[6]

        def sems(n, *names):
            return [[sem(f"{x}{i}") for i in range(n)] for x in names]

        edges_in, consts_in, bias_in, gate_bias_in, pad_zero = map(sem, ("edges_in", "consts_in", "bias_in", "gate_bias_in", "pad_zero"))
        (x_in,) = sems(3, "x_in")
        w_in, xn_stored, tok_rows_in, tok_bias_in = sems(2, "w_in", "xn_stored", "tok_rows_in", "tok_bias_in")
        (os_out,) = sems(4, "os_out")
        (rows_in,) = sems(RING, "rows_in")
        (moe_in,) = sems(NT, "moe_in")
        iota_done, consts_ready = sem("iota_done"), sem("consts_ready")
        stats_ready, std_ready, xn_ready = sem("stats_ready"), sem("std_ready"), sem("xn_ready")
        t_full, t_read = sem("t_full"), sem("t_read")
        a_full, a_read = sem("a_full"), sem("a_read")
        v_full, v_read = sem("v_full"), sem("v_read")
        dve_step = sem("dve_step")
        counts_ready = sem("counts_ready")
        perm_ready, perm_done = sem("perm_ready"), sem("perm_done")
        list_ready = sem("list_ready")
        at_ready, issued = sem("at_ready"), sem("issued")
        hot_ready, slot_added = sem("hot_ready"), sem("slot_added")
        slot_summed = sem("slot_summed")
        inv_ready, inv_stored = sem("inv_ready"), sem("inv_stored")
        inv_in, inv_kept, inv_listed = sem("inv_in"), sem("inv_kept"), sem("inv_listed")
        agg_ready, agg_t_ready = sem("agg_ready"), sem("agg_t_ready")
        gelu_b_ready, hidden_ready = sem("gelu_b_ready"), sem("hidden_ready")
        exp_in, exp_ready = sem("exp_in"), sem("exp_ready")
        act_turn = sem("act_turn")
        tanh_ready, mixed_ready = sem("tanh_ready"), sem("mixed_ready")
        tok_perm_ready, tok_list_ready = sem("tok_perm_ready"), sem("tok_list_ready")
        tok_bias_free = sem("tok_bias_free")
        tok_h_ready, tok_out_ready = sem("tok_h_ready"), sem("tok_out_ready")
        out_ready, out_done = sem("out_ready"), sem("out_done")
        block = ctx.enter_context(nc.Block())

        def rows_of(m):
            return P if m < NT - 1 else LAST

        def os_uses(k, n):
            return (n - k + 3) // 4

        def group_of(m):
            return m * P // HALF

        @block.sync
        def _(sp):
            for dst, src in ((e_dst, a["dst"]), (e_src, a["src"]), (e_typ, a["edge_type_8"]), (e_w, a["edge_weight"])):
                sp.dma_start(dst, src.rearrange("(p t) -> p t", t=ET)).then_inc(edges_in, 16)
            tiles = a["x"][0:(NT - 1) * P, :].rearrange("(m p) d -> p m d", p=P)
            for i in range(2):
                lo, hi = (0, 4) if i == 0 else (4, NT - 1)
                sp.dma_start(X[:, lo:hi, :], tiles[:, lo:hi, :]).then_inc(x_in[i], 16)
            sp.wait_ge(pad_zero, 1)
            sp.dma_start(X[0:LAST, NT - 1, :], a["x"][(NT - 1) * P:N_NODES, :]).then_inc(x_in[2], 16)

            def unit(u):
                return W[:, u % 2, :].rearrange("p (k n) -> p k n", k=8), w_in[u % 2]

            def wide(ap):
                return ap.rearrange("(k p) n -> p k n", p=P)

            w0, s0 = unit(UNIT_ENC)
            sp.dma_start(w0, wide(a["encT"])).then_inc(s0, 16)
            w1, s1 = unit(UNIT_CONVLIN)
            sp.dma_start(w1, wide(a["convlin"])).then_inc(s1, 16)
            for dst, src in (
                (b_enc[:], a["b_enc"]), (b_up[:], a["b_up"]), (b2_rows[:], a["L0_ffn_b2"]),
                (w_route[:], wide(a["L0_ffn_wr"])), (w_route2[:], wide(a["gate_wT"])),
                (b_route[:], a["L0_ffn_br"].partition_broadcast(P)),
                (b_route2[:, 0, :], a["L1_ffn_gate_b"].partition_broadcast(P)),
                (b_route2[:, 1, :], a["L1_ffn_expert_bias"].partition_broadcast(P)),
            ):
                sp.dma_start(dst, src).then_inc(consts_in, 16)
            sp.wait_ge(a_full, A_H2)
            dec = W[:, UNIT_DEC % 2, :].rearrange("p (k n) -> p k n", k=KE)
            sp.dma_start(dec, wide(a["decT"])).then_inc(w_in[UNIT_DEC % 2], 16)
            sp.wait_ge(slot_summed, RING + SLOTS)
            sp.dma_start(b_dec, a["L0_gnn_bdec"].partition_broadcast(P)).then_inc(bias_in, 16)
            with sp.Fori(0, E0) as e:
                u = UNIT_E0
                sp.wait_ge(a_full, KH * len(TOKG) * e + A_UP)
                w0, s0 = unit(u)
                src = a["L0_ffn_w1"][bass.ds(e, 1), :, :].rearrange("e (k p) n -> p (e k) n", p=P)
                sp.dma_start(w0, src).then_inc(s0, 16)
                sp.wait_ge(v_full, 2 * NT * e + V_DOWN)
                w1 = W[:, (u + 1) % 2, :].rearrange("p (k n) -> p k n", k=KH)
                src = a["L0_ffn_w2"][bass.ds(e, 1), :, :].rearrange("e (k p) n -> p (e k) n", p=P)
                sp.dma_start(w1, src).then_inc(w_in[(u + 1) % 2], 16)
            def relation(r, h):
                w0, s0 = unit(UNIT_REL + h)
                src = a["L1_gnn_weight"][bass.ds(r, 1), :, h * HALF:(h + 1) * HALF]
                sp.dma_start(w0, src.rearrange("r (k p) n -> p (r k) n", p=P)).then_inc(s0, 16)

            sp.wait_ge(a_full, A_Y)
            relation(0, 0)
            sp.wait_ge(v_full, V_CSUM)
            relation(0, 1)
            with sp.Fori(1, REL) as r:
                for h in range(2):
                    sp.wait_ge(a_full, 2 * NT * r + A_Y - NT * (1 - h))
                    relation(r, h)
            root = [a["L1_gnn_root"][:, h * HALF:(h + 1) * HALF] for h in range(2)]
            gate = [a["L1_gnn_w_gate"][b * D:(b + 1) * D, h * HALF:(h + 1) * HALF] for h in range(2) for b in range(2)]
            before_unit = [(a_full, A_Y + 2 * NT * REL - NT), (a_full, A_Y + 2 * NT * REL), (slot_summed, RING + 2 * SLOTS),
                           (slot_summed, RING + 2 * SLOTS), (v_full, V_GATE + NT), (v_full, V_GATE + NT)]
            for u, src, (done, n) in zip(range(UNIT_ROOT, UNIT_E1), root + gate, before_unit):
                if u == UNIT_ROOT:
                    sp.wait_ge(t_read, T_LN3 + 2 * NT)
                    sp.dma_start(b_rgcn, a["L1_gnn_bias"].partition_broadcast(P)).then_inc(bias_in, 16)
                if u == UNIT_GATE:
                    for k in range(4):
                        sp.wait_ge(os_out[k], 16 * os_uses(k, NT + 2 * NT * REL))
                    sp.dma_start(b_gate, a["L1_gnn_b_gate"].partition_broadcast(P)).then_inc(gate_bias_in, 16)
                sp.wait_ge(done, n)
                w0, s0 = unit(u)
                sp.dma_start(w0, wide(src)).then_inc(s0, 16)
            sp.wait_ge(tok_list_ready, 1)
            with sp.Fori(0, TSLOTS // 2) as i:
                for b in range(2):
                    e = sp.value_load(slot_exp[0:1, bass.ds(2 * i + b, 1)], min_val=0, max_val=E1 - 1)
                    u = UNIT_E1 + 2 * b
                    sp.wait_ge(v_full, 3 * (2 * i + b) + V_SLOT - 2)
                    w0, s0 = unit(u)
                    src = a["L1_ffn_w1"][bass.ds(e, 1), :, :].rearrange("e (k p) n -> p (e k) n", p=P)
                    sp.dma_start(w0, src).then_inc(s0, 16)
                    sp.wait_ge(tok_bias_free, 2 * i + b + 1)
                    sp.dma_start(tok_b1[:, b, :], a["L1_ffn_b1"][bass.ds(e, 1), :].rearrange("e n -> (e n)").partition_broadcast(P)).then_inc(tok_bias_in[b], 16)
                    sp.dma_start(tok_b2[:, b, :], a["L1_ffn_b2"][bass.ds(e, 1), :].rearrange("e n -> (e n)").partition_broadcast(P)).then_inc(tok_bias_in[b], 16)
                    sp.wait_ge(v_full, 3 * (2 * i + b) + V_SLOT)
                    w1 = W[:, (u + 1) % 2, :].rearrange("p (k n) -> p k n", k=KH)
                    src = a["L1_ffn_w2"][bass.ds(e, 1), :, :].rearrange("e (k p) n -> p (e k) n", p=P)
                    sp.dma_start(w1, src).then_inc(w_in[(u + 1) % 2], 16)
            for m in range(NT):
                sp.wait_ge(out_ready, m + 1)
                sp.dma_start(out[m * P:m * P + rows_of(m), :], X[0:rows_of(m), m, :]).then_inc(out_done, 16)
            sp.wait_ge(out_done, 16 * NT)

        @block.gpsimd
        def _(pool):
            pool.memset(X[96:P, NT - 1, :], 0.0).then_inc(pad_zero, 1)
            pool.wait_ge(pad_zero, 1)
            pool.iota(iota_free[:], [[1, SLOTS]], base=0, channel_multiplier=0,
                      allow_small_or_imprecise_dtypes=True).then_inc(iota_done, 1)
            pool.wait_ge(iota_done, 1)
            pool.iota(iota_part[:], [[0, 1]], base=0, channel_multiplier=1,
                      allow_small_or_imprecise_dtypes=True).then_inc(iota_done, 1)
            pool.wait_ge(iota_done, 2)
            pool.iota(tok_id[:], [[P, NT]], base=0, channel_multiplier=1,
                      allow_small_or_imprecise_dtypes=True).then_inc(iota_done, 1)
            pool.wait_ge(iota_done, 3)
            pool.memset(ident[:], 0.0).then_inc(iota_done, 1)
            pool.wait_ge(iota_done, 4)
            pool.affine_select(out=ident[:], in_=ident[:], compare_op=ALU.not_equal, fill=1.0, base=0,
                               pattern=[[-1, P]], channel_multiplier=1).then_inc(iota_done, 1)

            def gather_slots(table, at_list, rows, done, rounds_done):
                with pool.Fori(0, SLOTS // (2 * RING)) as i:
                    for half in range(2):
                        pool.tensor_copy(at_ring[:, half, :], at_list[:, bass.ds(2 * RING * i + half * RING, RING)]).then_inc(at_ready, 1)
                        for k in range(RING):
                            if k % BATCH == 0:
                                pool.wait_ge(slot_summed, done + 2 * RING * i + half * RING + k + BATCH)
                                pool.sem_inc(issued, 1)
                            if k == 0:
                                pool.wait_ge(at_ready, rounds_done + 2 * i + half + 1)
                                pool.sem_inc(issued, 1)
                            pool.indirect_dma_start(rows(k), None, table,
                                                    bass.IndirectOffsetOnAxis(ap=at_ring[:, half, k:k + 1], axis=0)
                                                    ).then_inc(rows_in[k], 16)

            pool.wait_ge(list_ready, 1)
            for k in range(4):
                pool.wait_ge(os_out[k], 16 * os_uses(k, NT))
            gather_slots(h2_dram, l_src, lambda k: rows_h2[:, k, :], 0, 0)

            pool.wait_ge(inv_stored, 16)
            pool.wait_ge(rows_in[RING - 1], 16 * SLOTS // RING)
            inv_rows = inv_dram.rearrange("n (r o) -> (n r) o", o=1)
            with pool.Fori(0, SLOTS // RING) as i:
                pool.tensor_copy(at_ring[:, 0, :], l_inv_at[:, bass.ds(RING * i, RING)]).then_inc(at_ready, 1)
                pool.wait_ge(at_ready, SLOTS // RING + i + 1)
                pool.sem_inc(issued, 1)
                for k in range(RING):
                    pool.indirect_dma_start(inv_ring[:, k:k + 1], None, inv_rows,
                                            bass.IndirectOffsetOnAxis(ap=at_ring[:, 0, k:k + 1], axis=0)
                                            ).then_inc(inv_in, 16)
                pool.wait_ge(inv_in, 16 * RING * (i + 1))
                pool.sem_inc(issued, 1)
                pool.tensor_copy(l_inv[:, bass.ds(RING * i, RING)], inv_ring[:, :]).then_inc(inv_kept, 1)
                pool.wait_ge(inv_kept, i + 1)
                pool.sem_inc(issued, 1)
            pool.sem_inc(inv_listed, 1)

            for k in range(4):
                pool.wait_ge(os_out[k], 16 * os_uses(k, NT + 2 * NT * REL))
            pool.wait_ge(v_full, V_GATE)
            gather_slots(y_dram.rearrange("n r d -> (n r) d"), l_row8, lambda k: rows_y[:, k, :], SLOTS, 2 * SLOTS // RING)

            pool.wait_ge(tok_list_ready, 1)
            for b in range(2):
                pool.wait_ge(xn_stored[b], 16 * NT // 2)
            rounds = 3 * SLOTS // RING
            with pool.Fori(0, TSLOTS // 2) as i:
                for b in range(2):
                    pool.wait_ge(t_full, T_SLOT + 3 * (2 * i + b) - 4)
                    pool.sem_inc(issued, 1)
                    pool.tensor_copy(at_ring[:, 0, b:b + 1], tok_list[:, bass.ds(2 * i + b, 1)]).then_inc(at_ready, 1)
                    pool.wait_ge(at_ready, rounds + 2 * i + b + 1)
                    pool.sem_inc(issued, 1)
                    pool.indirect_dma_start(tok_rows[:, b, :], None, xn_dram,
                                            bass.IndirectOffsetOnAxis(ap=at_ring[:, 0, b:b + 1], axis=0)
                                            ).then_inc(tok_rows_in[b], 16)
            total = NT + 2 * NT * REL + 2 * TSLOTS
            for k in range(4):
                pool.wait_ge(os_out[k], 16 * os_uses(k, total))
            for m in range(NT):
                pool.indirect_dma_start(moe_rows[0:rows_of(m), m, :], None, moe_dram,
                                        bass.IndirectOffsetOnAxis(ap=tok_posi[0:rows_of(m), m:m + 1], axis=0)
                                        ).then_inc(moe_in[m], 16)

        @block.tensor
        def _(pe):
            mm = nc.tensor.matmul
            pe.sem_inc(slot_summed, RING)

            def unit(u, wide=8):
                return W[:, u % 2, :].rearrange("p (k n) -> p k n", k=wide)

            def uses(u):
                return u // 2 + 1

            def transpose4(n, blocks):
                pe.wait_ge(t_read, n - 1) if not isinstance(n, int) or n >= 2 else None
                for j, blk in enumerate(blocks):
                    last = nc.tensor.transpose(t_bank[t_slot(n)][:, j * P:(j + 1) * P], blk, ident[:])
                return last.then_inc(t_full, 1)

            def t_slot(n):
                return n % 2

            def transpose_x(base):
                for m in range(NT):
                    pe.wait_ge(xn_ready, (base_ln[base]) * NT + m + 1)
                    for j in range(2):
                        transpose4(base + 2 * m + j, [XN[:, m % 2, (4 * j + q) * P:(4 * j + q + 1) * P] for q in range(4)])

            base_ln = {T_LN1: 0, T_LN2: 1, T_LN3: 2, T_LN4: 3}

            pe.wait_ge(consts_ready, 1)
            pe.wait_ge(counts_ready, 1)
            mm(v_bank[0][:, 0:NT], before[:], pre[:, 1, :], start=True, stop=True)
            mm(v_bank[0][:, 16:16 + NT], ones[:], pre[:, 1, :], start=True, stop=True).then_inc(v_full, 1)
            transpose_x(T_LN1)

            pe.wait_ge(w_in[0], 16)
            w = unit(UNIT_ENC)
            for g, (lo, n) in enumerate(TOKG):
                pe.wait_ge(t_read, T_LN1 + 2 * min(NT, (lo + n) // P))
                for c in range(KE):
                    q = A_ENC + g * KE + c
                    if q >= 2:
                        pe.wait_ge(a_read, q - 1)
                    for k in range(KD):
                        last = mm(a_bank[q % 2][:, 0:n], w[:, k, c * P:(c + 1) * P], XT[:, k, lo:lo + n],
                                  start=(k == 0), stop=(k == KD - 1))
                    last.then_inc(a_full, 1)
            last_enc = A_ENC + KE * len(TOKG)

            pe.wait_ge(w_in[1], 16)
            pe.wait_ge(a_read, last_enc)
            w = unit(UNIT_CONVLIN)

            def from_h(base, k0):
                for m in range(NT):
                    q = base + m
                    pe.wait_ge(a_read, q - 1)
                    for k in range(KE):
                        last = mm(a_bank[q % 2][:], hT[:, k, m * P:(m + 1) * P], w[:, k0 + k, :],
                                  start=(k == 0), stop=(k == KE - 1))
                    last.then_inc(a_full, 1)

            from_h(A_H2, 0)

            def permute(t, k, first=False, final=False):
                pe.wait_ge(perm_ready, t + 1)
                mm(list_bank[:, 0:2 * SLOTS], perm_lane[:, k, :], perm_val[:, k, :],
                   start=first, stop=final).then_inc(perm_done, 1)

            head, tail = 3, (ET - 3) % 4 or 4
            for t in range(head):
                permute(t, t % 4, first=(t == 0))
            with pe.Fori(0, (ET - head - tail) // 4) as i:
                for j in range(4):
                    permute(4 * i + head + j, (head + j) % 4)
            for t in range(ET - tail, ET):
                permute(t, t % 4, final=(t == ET - 1))
            from_h(A_LIN, KE)

            def slot_sum(i, k, first=False):
                if not first or k >= 4:
                    pe.wait_ge(slot_added, RING * i + (k - 3))
                pe.wait_ge(hot_ready, RING * i + k + 1)
                pe.wait_ge(rows_in[k], 16 * i + 16)
                mm(sum_bank[k % 4][:, EMBC:EMBP], hot1[:, k, :], hotr[:, k, :], start=True, stop=True)
                mm(sum_bank[k % 4][:, 0:EMBC], hot[:, k, :], rows_h2[:, k, 0:EMBC], start=True, stop=True).then_inc(slot_summed, 1)

            for k in range(RING):
                slot_sum(0, k, first=True)
            with pe.Fori(1, SLOTS // RING) as i:
                for k in range(RING):
                    slot_sum(i, k)

            pe.wait_ge(agg_ready, 1)
            pe.wait_ge(w_in[0], 16 * uses(UNIT_DEC))
            w = unit(UNIT_DEC, KE)
            for m in range(NT + 1):
                if m < NT:
                    transpose4(T_AGG + m, [agg[:, m, c * P:(c + 1) * P] for c in range(KE)])
                if m >= 1:
                    pe.wait_ge(t_read, T_AGG + m)
                    for h in range(2):
                        q = V_DEC + 2 * (m - 1) + h
                        pe.wait_ge(v_read, q - 1)
                        for k in range(KE):
                            last = mm(v_bank[q % 2][:], hT[:, k, (m - 1) * P:m * P], w[:, k, h * HALF:(h + 1) * HALF],
                                      start=(k == 0), stop=(k == KE - 1))
                        last.then_inc(v_full, 1)

            def route(q, weights, n):
                pe.wait_ge(v_read, q - 1)
                for m in range(NT):
                    for k in range(KD):
                        last = mm(v_bank[q % 2][:, m * 8:m * 8 + n], XT[:, k, m * P:(m + 1) * P], weights[:, k, :],
                                  start=(k == 0), stop=(k == KD - 1))
                last.then_inc(v_full, 1)

            transpose_x(T_LN2)
            pe.wait_ge(t_read, T_LN2 + 2 * NT)
            pe.wait_ge(consts_in, 16 * 8)
            route(V_ROUTE, w_route, E0)
            with pe.Fori(0, E0) as e:
                u = UNIT_E0
                w = unit(u)
                pe.wait_ge(w_in[u % 2], 16 * e + 16 * uses(u))
                for g, (lo, n) in enumerate(TOKG):
                    for c in range(KH):
                        j = g * KH + c
                        pe.wait_ge(a_read, KH * len(TOKG) * e + A_UP + j - 1)
                        for k in range(KD):
                            last = mm(a_bank[(A_UP + j) % 2][:, 0:n], w[:, k, c * P:(c + 1) * P], XT[:, k, lo:lo + n],
                                      start=(k == 0), stop=(k == KD - 1))
                        last.then_inc(a_full, 1)
                w = unit(u + 1, KH)
                pe.wait_ge(w_in[(u + 1) % 2], 16 * e + 16 * uses(u + 1))
                for m in range(NT):
                    if m == 0 or group_of(m) != group_of(m - 1):
                        pe.wait_ge(hidden_ready, 16 * e + (4, 8, 16)[group_of(m)])
                    for h in range(2):
                        j = 2 * m + h
                        pe.wait_ge(v_read, 2 * NT * e + V_DOWN + j - 1)
                        for k in range(KH):
                            last = mm(v_bank[(V_DOWN + j) % 2][:], hT[:, k, m * P:(m + 1) * P], w[:, k, h * HALF:(h + 1) * HALF],
                                      start=(k == 0), stop=(k == KH - 1))
                        last.then_inc(v_full, 1)
            pe.wait_ge(v_read, V_CSUM)
            for h in range(2):
                cols = slice(h * HALF, (h + 1) * HALF)
                mm(v_bank[(V_CSUM + h) % 2][:], sel_sum[:], X[:, NT - 1, cols], start=True, stop=False)
                mm(v_bank[(V_CSUM + h) % 2][:], ones[0:E0, :], b2_rows[:, cols], start=False, stop=True).then_inc(v_full, 1)

            transpose_x(T_LN3)
            pe.wait_ge(t_read, T_LN3 + 2 * NT)
            with pe.Fori(0, REL) as r:
                for h in range(2):
                    u = UNIT_REL + h
                    w = unit(u)
                    pe.wait_ge(w_in[u % 2], 16 * r + 16 * uses(u))
                    for m in range(NT):
                        j = h * NT + m
                        pe.wait_ge(a_read, 2 * NT * r + A_Y + j - 1)
                        for k in range(KD):
                            last = mm(a_bank[(A_Y + j) % 2][:], XT[:, k, m * P:(m + 1) * P], w[:, k, :],
                                      start=(k == 0), stop=(k == KD - 1))
                        last.then_inc(a_full, 1)
            for h in range(2):
                u = UNIT_ROOT + h
                w = unit(u)
                pe.wait_ge(w_in[u % 2], 16 * uses(u))
                for m in range(NT):
                    q = V_ROOT + h * NT + m
                    pe.wait_ge(v_read, q - 1)
                    for k in range(KD):
                        last = mm(v_bank[q % 2][:], XT[:, k, m * P:(m + 1) * P], w[:, k, :],
                                  start=(k == 0), stop=(k == KD - 1))
                    last.then_inc(v_full, 1)

            pe.wait_ge(v_read, V_GATE)

            def slot_sum2(i, k, first=False):
                done = SLOTS + RING * i + k
                if not first or k >= 4:
                    pe.wait_ge(slot_added, done - 3)
                pe.wait_ge(hot_ready, done + 1)
                pe.wait_ge(rows_in[k], 16 * i + 16 * (SLOTS // RING) + 16)
                pair = pairs[(k + 1) % 4]
                mm(pair[:, 0:HALF], hot[:, k, :], rows_y[:, k, 0:HALF], start=True, stop=True)
                mm(pair[:, HALF:D], hot[:, k, :], rows_y[:, k, HALF:D], start=True, stop=True).then_inc(slot_summed, 1)

            for k in range(RING):
                slot_sum2(0, k, first=True)
            with pe.Fori(1, SLOTS // RING) as i:
                for k in range(RING):
                    slot_sum2(i, k)

            pe.wait_ge(agg_ready, 2)

            def transpose_u(n):
                m = n % NT
                for j in range(2):
                    transpose4(T_U + 2 * n + j, [u_rows[:, m, (4 * j + q) * P:(4 * j + q + 1) * P] for q in range(4)])

            transpose_u(0)
            for n in range(2 * NT):
                h, m = divmod(n, NT)
                if n + 1 < 2 * NT:
                    transpose_u(n + 1)
                top_u, bottom_u = UNIT_GATE + 2 * h, UNIT_GATE + 2 * h + 1
                if m == 0:
                    pe.wait_ge(w_in[top_u % 2], 16 * uses(top_u))
                    pe.wait_ge(w_in[bottom_u % 2], 16 * uses(bottom_u))
                pe.wait_ge(t_read, T_U + 2 * n + 2)
                q = V_GATE + n
                pe.wait_ge(v_read, q - 1)
                for k in range(KD):
                    mm(v_bank[q % 2][:], uT[:, n % 2, k, :], unit(top_u)[:, k, :], start=(k == 0), stop=False)
                for k in range(KD):
                    last = mm(v_bank[q % 2][:], XT[:, k, m * P:(m + 1) * P], unit(bottom_u)[:, k, :],
                              start=False, stop=(k == KD - 1))
                last.then_inc(v_full, 1)

            transpose_x(T_LN4)
            pe.wait_ge(t_read, T_LN4 + 2 * NT)
            route(V_ROUTE2, w_route2, E1)
            pe.wait_ge(counts_ready, 2)
            pe.wait_ge(v_read, V_PRE2 - 1)
            b = v_bank[V_PRE2 % 2]
            mm(b[:, 0:E1], before[:], pre[:, 1, 0:E1], start=True, stop=True)
            mm(b[:, 16:16 + E1], ones[:], pre[:, 1, 0:E1], start=True, stop=True).then_inc(v_full, 1)
            pe.wait_ge(tok_perm_ready, 1)
            pe.wait_ge(v_read, V_LIST2 - 1)
            for t in range(NT):
                last = mm(v_bank[V_LIST2 % 2][:, 0:TSLOTS], tok_perm_lane[:, t, :], tok_perm_val[:, t, :],
                          start=(t == 0), stop=(t == NT - 1))
            last.then_inc(v_full, 1)

            def transpose_rows(n, b):
                for j in range(2):
                    pe.wait_ge(t_read, n + j - 1)
                    for q in range(4):
                        last = nc.tensor.transpose(t_bank[(3 * b + T_SLOT + j) % 2][:, q * P:(q + 1) * P],
                                                   tok_rows[:, b, (4 * j + q) * P:(4 * j + q + 1) * P], ident[:])
                    last.then_inc(t_full, 1)

            def tok_slot_step(i, b, final=False):
                s = 2 * i + b
                u = UNIT_E1 + 2 * b
                w = unit(u)
                pe.wait_ge(w_in[u % 2], 32 * i + 16 * uses(u))
                pe.wait_ge(t_read, 3 * s + T_SLOT + 2)
                pe.wait_ge(v_read, 3 * s + V_SLOT - 1)
                for k in range(KD):
                    last = mm(v_bank[(3 * b + V_SLOT) % 2][:], tok_xT[:, b, k, :], w[:, k, :],
                              start=(k == 0), stop=(k == KD - 1))
                last.then_inc(v_full, 1)
                if not final:
                    pe.wait_ge(tok_rows_in[1 - b], 16 * i + 16 * (b + 1))
                    for j in range(2):
                        n = 3 * s + T_SLOT + 2 + j
                        pe.wait_ge(t_read, n - 1)
                        for q in range(4):
                            last = nc.tensor.transpose(t_bank[(3 * b + T_SLOT + 2 + j) % 2][:, q * P:(q + 1) * P],
                                                       tok_rows[:, 1 - b, (4 * j + q) * P:(4 * j + q + 1) * P], ident[:])
                        last.then_inc(t_full, 1)
                skip = 2 if final else 0
                pe.wait_ge(tok_h_ready, s + 1)
                n = 3 * s + T_SLOT + 4 - skip
                pe.wait_ge(t_read, n - 1)
                for q in range(KH):
                    last = nc.tensor.transpose(t_bank[(3 * b + T_SLOT + 4) % 2][:, q * P:(q + 1) * P],
                                               tok_h[:, b, q * P:(q + 1) * P], ident[:])
                last.then_inc(t_full, 1)
                w = unit(u + 1, KH)
                pe.wait_ge(w_in[(u + 1) % 2], 32 * i + 16 * uses(u + 1))
                pe.wait_ge(t_read, n + 1)
                for h in range(2):
                    pe.wait_ge(v_read, 3 * s + V_SLOT + h)
                    for k in range(KH):
                        last = mm(v_bank[(3 * b + V_SLOT + 1 + h) % 2][:], tok_hT[:, b, k, :], w[:, k, h * HALF:(h + 1) * HALF],
                                  start=(k == 0), stop=(k == KH - 1))
                    last.then_inc(v_full, 1)

            pe.wait_ge(tok_rows_in[0], 16)
            transpose_rows(T_SLOT, 0)
            with pe.Fori(0, TSLOTS // 2 - 1) as i:
                for b in range(2):
                    tok_slot_step(i, b)
            tok_slot_step(TSLOTS // 2 - 1, 0)
            tok_slot_step(TSLOTS // 2 - 1, 1, final=True)

        @block.scalar
        def _(act):
            def copy(dst, src, func=ACT.Copy, **kw):
                return nc.scalar.activation(dst, src, func, **kw)

            def take_xT(base):
                for m in range(NT):
                    for j in range(2):
                        n = base + 2 * m + j
                        act.wait_ge(t_full, n + 1)
                        copy(XT[:, 4 * j:4 * j + 4, m * P:(m + 1) * P],
                             t_bank[n % 2][:].rearrange("p (q n) -> p q n", q=4)).then_inc(t_read, 1)

            def roots(n):
                act.wait_ge(stats_ready, n)
                nc.scalar.activation(std[:], mv[:, :, 1], ACT.Sqrt, bias=eps[:]).then_inc(std_ready, 1)

            roots(1)
            take_xT(T_LN1)
            act.wait_ge(consts_in, 16 * 8)
            for g, (lo, n) in enumerate(TOKG):
                for c in range(KE):
                    q = A_ENC + g * KE + c
                    act.wait_ge(a_full, q + 1)
                    nc.scalar.activation(hT[:, c, lo:lo + n], a_bank[q % 2][:, 0:n], ACT.Sigmoid,
                                         bias=b_enc[:, c:c + 1]).then_inc(a_read, 1)
            for m in range(NT):
                q, k = A_H2 + m, m % 4
                act.wait_ge(a_full, q + 1)
                if m >= 4:
                    act.wait_ge(os_out[k], 16 * (m // 4))
                copy(OS[:, k, :], a_bank[q % 2][:]).then_inc(a_read, 1)
                act.wait_ge(a_read, q + 1)
                act.dma_start(h2_dram[m * P:(m + 1) * P, :], OS[:, k, :]).then_inc(os_out[k], 16)
            for m in range(NT):
                q = A_LIN + m
                act.wait_ge(a_full, q + 1)
                if m == 0:
                    act.wait_ge(perm_done, ET)
                copy(agg[:, m, :], a_bank[q % 2][:]).then_inc(a_read, 1)

            act.wait_ge(inv_ready, 1)
            act.dma_start(inv_dram.rearrange("(m p) r -> p m r", p=P), count[:]).then_inc(inv_stored, 16)

            for m in range(NT):
                n = T_AGG + m
                act.wait_ge(t_full, n + 1)
                copy(hT[:, :, m * P:(m + 1) * P], t_bank[n % 2][:].rearrange("p (q n) -> p q n", q=4)).then_inc(t_read, 1)

            roots(2)
            take_xT(T_LN2)
            nc.scalar.activation(g_up[:], b_up[:], ACT.Gelu).then_inc(gelu_b_ready, 1)
            act.wait_ge(exp_in, 1)
            nc.scalar.activation(gsm[:, 1, :], gsm[:, 0, :], ACT.Exp).then_inc(exp_ready, 1)
            with act.Fori(0, E0) as e:
                for g, (lo, n) in enumerate(TOKG):
                    for c in range(KH):
                        j = g * KH + c
                        act.wait_ge(a_full, KH * len(TOKG) * e + A_UP + j + 1)
                        act.sem_inc(act_turn, 1)
                        nc.scalar.activation(hT[:, c, lo:lo + n], a_bank[(A_UP + j) % 2][:, 0:n], ACT.Gelu,
                                             bias=b_up[:, bass.ds(KH * e + c, 1)]).then_inc(a_read, 1)

            roots(3)
            take_xT(T_LN3)
            with act.Fori(0, REL) as r:
                for h in range(2):
                    for m in range(NT):
                        j = h * NT + m
                        n = NT + j
                        k = n % 4
                        act.wait_ge(os_out[k], 16 * (2 * NT // 4) * r + 16 * (n // 4))
                        act.wait_ge(a_full, 2 * NT * r + A_Y + j + 1)
                        copy(OS[:, k, :], a_bank[(A_Y + j) % 2][:]).then_inc(a_read, 1)
                        act.wait_ge(a_read, 2 * NT * r + A_Y + j + 1)
                        act.dma_start(y_dram[m * P:(m + 1) * P, bass.ds(r, 1), h * HALF:(h + 1) * HALF],
                                      OS[:, k:k + 1, :]).then_inc(os_out[k], 16)
            for n in range(2 * NT):
                h, m = divmod(n, NT)
                for j in range(2):
                    q = T_U + 2 * n + j
                    act.wait_ge(t_full, q + 1)
                    if n >= 2:
                        act.wait_ge(v_full, V_GATE + n - 1)
                    copy(uT[:, n % 2, 4 * j:4 * j + 4, :], t_bank[q % 2][:].rearrange("p (q n) -> p q n", q=4)).then_inc(t_read, 1)
                if n >= 2:
                    act.wait_ge(mixed_ready, n - 1)
                nc.scalar.activation(mixed[:, n % 2, :], u_rows[:, m, h * HALF:(h + 1) * HALF], ACT.Tanh).then_inc(tanh_ready, 1)

            roots(4)
            for m in range(NT):
                act.wait_ge(xn_ready, 3 * NT + m + 1)
                act.dma_start(xn_dram[m * P:(m + 1) * P, :], XN[:, m % 2, :]).then_inc(xn_stored[m % 2], 16)
                for j in range(2):
                    n = T_LN4 + 2 * m + j
                    act.wait_ge(t_full, n + 1)
                    copy(XT[:, 4 * j:4 * j + 4, m * P:(m + 1) * P],
                         t_bank[n % 2][:].rearrange("p (q n) -> p q n", q=4)).then_inc(t_read, 1)

            def take(n, parity, dst, func=ACT.Copy):
                act.wait_ge(t_full, n + 1)
                copy(dst, t_bank[parity][:].rearrange("p (q n) -> p q n", q=4), func).then_inc(t_read, 1)

            def slot_out(i, b):
                for h in range(2):
                    n = NT + 2 * NT * REL + 2 * b + h
                    k = n % 4
                    act.wait_ge(tok_out_ready, 4 * i + 2 * b + h + 1)
                    act.dma_start(moe_dram.rearrange("(s p) d -> s p d", p=P)[bass.ds(2 * i + b, 1), :, h * HALF:(h + 1) * HALF].rearrange("s p d -> p s d"),
                                  OS[:, k:k + 1, :]).then_inc(os_out[k], 16)

            def tok_slot_step(i, b, final=False):
                s = 2 * i + b
                if not final:
                    for j in range(2):
                        take(3 * s + T_SLOT + 2 + j, (3 * b + T_SLOT + 2 + j) % 2, tok_xT[:, 1 - b, 4 * j:4 * j + 4, :])
                skip = 2 if final else 0
                take(3 * s + T_SLOT + 4 - skip, (3 * b + T_SLOT + 4) % 2, tok_hT[:, b, :, :], ACT.Relu)
                slot_out(i, b)

            for j in range(2):
                take(T_SLOT + j, (T_SLOT + j) % 2, tok_xT[:, 0, 4 * j:4 * j + 4, :])
            with act.Fori(0, TSLOTS // 2 - 1) as i:
                for b in range(2):
                    tok_slot_step(i, b)
            tok_slot_step(TSLOTS // 2 - 1, 0)
            tok_slot_step(TSLOTS // 2 - 1, 1, final=True)

        @block.vector
        def _(dve):
            v = nc.vector
            steps = [0]

            def link(ins):
                steps[0] += 1
                ins.then_inc(dve_step, 1)
                dve.wait_ge(dve_step, steps[0])

            def ln_stats(m):
                for h in range(2):
                    last = v.bn_stats(stats[:, m % 2, h, :], X[:, m, h * HALF:(h + 1) * HALF])
                link(last)
                return v.bn_aggr(mv[:, m, :], stats[:, m % 2, :, :].rearrange("p a b -> p (a b)"))

            def normalise(n, base, stored=False):
                dve.wait_ge(std_ready, n)
                link(v.reciprocal(rstd[:], std[:]))
                for m in range(NT):
                    if m >= 2:
                        dve.wait_ge(t_full, base + 2 * m - 2)
                        if stored:
                            dve.wait_ge(xn_stored[m % 2], 16 * (m // 2))
                    v.tensor_scalar(XN[:, m % 2, :], X[:, m, :], mv[:, m, 0:1], rstd[:, m:m + 1],
                                    ALU.subtract, ALU.mult).then_inc(xn_ready, 1)

            def sort(key, groups, cols, onehot, cum, pos, bank, full, tmp):
                gs = slice(0, groups)
                for g in range(groups):
                    last = v.tensor_scalar(onehot[:, g * cols:(g + 1) * cols], key, float(g), None, ALU.is_equal)
                link(last)
                link(v.tensor_tensor_scan(cum, onehot, onehot, 0.0, ALU.add, ALU.max))
                ends = cum.rearrange("p (g t) -> p g t", t=cols)[:, :, cols - 1]
                v.memset(pre[:, 2, 0:1], 0.0)
                v.tensor_copy(pre[:, 2, 1:groups], ends[:, 0:groups - 1])
                link(v.tensor_copy(pre[:, 0, gs], ends))
                v.tensor_tensor(pre[:, 1, gs], pre[:, 0, gs], pre[:, 2, gs], ALU.subtract).then_inc(counts_ready, 1)
                dve.wait_ge(v_full, full + 1)
                link(v.tensor_scalar(prei[:, 0, gs], bank[:, 16:16 + groups], float(P - 1), None, ALU.add))
                link(v.tensor_scalar(prei[:, 1, gs], prei[:, 0, gs], 7, None, ALU.arith_shift_right))
                link(v.tensor_copy(pre[:, 4, gs], prei[:, 1, gs]))
                link(v.tensor_tensor_scan(pre[:, 5, gs], pre[:, 4, gs], pre[:, 4, gs], 0.0, ALU.add, ALU.max))
                link(v.tensor_tensor(pre[:, 6, gs], pre[:, 5, gs], pre[:, 4, gs], ALU.subtract))
                link(v.scalar_tensor_tensor(pre[:, 7, gs], pre[:, 6, gs], float(P), bank[:, 0:groups], ALU.mult, ALU.add))
                v.sem_inc(v_read, 1)
                link(v.scalar_tensor_tensor(pre[:, 3, gs], pre[:, 7, gs], 1.0, pre[:, 2, gs], ALU.subtract, ALU.subtract))
                for g in range(groups):
                    part = slice(g * cols, (g + 1) * cols)
                    last = v.scalar_tensor_tensor(onehot[:, part], cum[:, part], pre[:, 3, g:g + 1], onehot[:, part], ALU.add, ALU.mult)
                v.tensor_scalar(tmp, key, float(groups), NOWHERE, ALU.is_ge, ALU.mult)
                link(last)
                link(v.tensor_reduce(pos, onehot.rearrange("p (g t) -> p t g", t=cols), AX.X, ALU.add))
                link(v.tensor_tensor(pos, pos, tmp, ALU.add))

            def slot_groups(out_i, tmp, n, groups):
                link(v.tensor_scalar(tmp, iota_free[:, 0:n], pre[:, 5, 0:1], None, ALU.is_ge))
                for g in range(1, groups):
                    link(v.scalar_tensor_tensor(tmp, iota_free[:, 0:n], pre[:, 5, g:g + 1], tmp, ALU.is_ge, ALU.add))
                link(v.tensor_scalar(out_i, tmp, float(groups - 1), None, ALU.min))

            v.memset(ones[:], 1.0)
            v.memset(eps[:], EPS)
            v.memset(logits[:], -3.0e38)
            link(v.memset(room[:], 0.0))
            dve.wait_ge(iota_done, 5)
            v.tensor_scalar(before[:], iota_free[:, 0:P], iota_part[:, 0:1], None, ALU.is_gt)
            v.tensor_scalar(pad_mask[:, 2:3], iota_part[:], float(SUMROW), None, ALU.is_lt)
            link(v.tensor_scalar(pad_mask[:, 0:1], iota_part[:], float(SUMROW), None, ALU.is_equal))
            v.tensor_scalar(sel_sum[:], ones[:], pad_mask[:, 0:1], None, ALU.mult)
            v.tensor_scalar(tok_pad[:], tok_id[:], float(N_NODES), 100.0, ALU.is_ge, ALU.mult)
            v.tensor_scalar(pad_mask[:, 1:2], pad_mask[:, 0:1], -1.0, 1.0, ALU.mult, ALU.add).then_inc(consts_ready, 1)

            dve.wait_ge(edges_in, 64)
            v.tensor_scalar(e_t1, e_dst, P - 1, None, ALU.bitwise_and)
            link(v.tensor_scalar(e_t0, e_dst, 7, None, ALU.arith_shift_right))
            link(v.tensor_copy(e_key, e_t0))
            sort(e_key, NT, ET, e_hot, e_cum, e_pos, v_bank[0], V_PRE, e_lane)
            slot_groups(l_tile[:], l_tmp[:], SLOTS, NT)
            for m in range(NT):
                if m in (0, 4, NT - 1):
                    dve.wait_ge(x_in[(0, 4, NT - 1).index(m)], 16)
                last = ln_stats(m)
            last.then_inc(stats_ready, 1)
            link(v.tensor_copy(e_t0, e_pos))
            link(v.tensor_scalar(e_dst, e_t0, P - 1, None, ALU.bitwise_and))
            link(v.tensor_copy(e_lane, e_dst))
            link(v.tensor_scalar(e_dst, e_t0, 7, None, ALU.arith_shift_right))
            link(v.tensor_copy(e_slot, e_dst))
            link(v.scalar_tensor_tensor(e_pack, e_src, float(REL), e_typ, ALU.mult, ALU.add))
            link(v.tensor_scalar(e_pos, e_t1, 1.0, float(1 << ROWSHIFT), ALU.add, ALU.mult))
            link(v.tensor_tensor(e_pack, e_pack, e_pos, ALU.add))
            normalise(1, T_LN1)

            def permute(t, k, first=False):
                if not first:
                    dve.wait_ge(perm_done, t - 3)
                col = (lambda ap: ap[:, t:t + 1]) if isinstance(t, int) else (lambda ap: ap[:, bass.ds(t, 1)])
                v.tensor_scalar(perm_lane[:, k, :], iota_free[:, 0:P], col(e_lane), None, ALU.is_equal)
                v.tensor_scalar(perm_val[:, k, 0:SLOTS], iota_free[:], col(e_slot), col(e_pack), ALU.is_equal, ALU.mult)
                v.tensor_scalar(perm_val[:, k, SLOTS:2 * SLOTS], iota_free[:], col(e_slot), col(e_w), ALU.is_equal,
                                ALU.mult).then_inc(perm_ready, 1)

            head = 4
            tail = (ET - head) % 4
            for t in range(head):
                permute(t, t % 4, first=True)
            with dve.Fori(0, (ET - head - tail) // 4) as i:
                for j in range(4):
                    permute(4 * i + head + j, j)
            for t in range(ET - tail, ET):
                permute(t, t % 4)
            dve.wait_ge(perm_done, ET)
            v.tensor_copy(l_w[:], list_bank[:, SLOTS:2 * SLOTS])
            link(v.tensor_copy(l_pack[:], list_bank[:, 0:SLOTS]))
            link(v.tensor_scalar(l_row8[:], l_pack[:], (1 << ROWSHIFT) - 1, None, ALU.bitwise_and))
            link(v.tensor_scalar(l_src[:], l_row8[:], RELBITS, None, ALU.arith_shift_right))
            link(v.tensor_scalar(l_inv_at[:], l_row8[:], REL - 1, None, ALU.bitwise_and))
            link(v.tensor_copy(l_rel[:], l_inv_at[:]))
            link(v.tensor_scalar(l_inv_at[:], l_pack[:], ROWSHIFT, None, ALU.arith_shift_right))
            link(v.tensor_scalar(l_row[:], l_inv_at[:], 1.0, None, ALU.subtract))
            link(v.tensor_scalar(l_tmp[:], l_row[:], 0.0, None, ALU.max))
            link(v.scalar_tensor_tensor(l_tmp[:], l_tile[:], float(P), l_tmp[:], ALU.mult, ALU.add))
            link(v.scalar_tensor_tensor(l_inv_at[:], l_tmp[:], float(REL), l_rel[:], ALU.mult, ALU.add))
            v.sem_inc(list_ready, 1)

            def make_hot(i, k, weight, base, counts):
                col = (lambda ap: ap[:, k:k + 1]) if isinstance(i, int) else (lambda ap: ap[:, bass.ds(RING * i + k, 1)])
                if counts:
                    v.tensor_scalar(hot1[:, k, :], iota_free[:, 0:P], col(l_row), None, ALU.is_equal)
                    v.tensor_scalar(hotr[:, k, :], iota_free[:, 0:REL], col(l_rel), None, ALU.is_equal)
                v.tensor_scalar(hot[:, k, :], iota_free[:, 0:P], col(l_row), col(weight), ALU.is_equal, ALU.mult).then_inc(hot_ready, 1)

            def add_slot(i, k):
                t = dve.value_load(l_tile[0:1, bass.ds(RING * i + k, 1)], min_val=0, max_val=NT - 1)
                dve.wait_ge(slot_summed, RING * i + (RING + k + 1))
                dve.wait_ge(slot_added, RING * i + k)
                v.tensor_tensor(agg[:, bass.ds(t, 1), :], sum_bank[k % 4][:].rearrange("p (o n) -> p o n", o=1),
                                agg[:, bass.ds(t, 1), :], ALU.add).then_inc(slot_added, 1)

            for k in range(RING):
                make_hot(0, k, l_w, 0, True)
            dve.wait_ge(a_read, A_LIN + NT)
            with dve.Fori(0, SLOTS // RING - 1) as i:
                for k in range(RING):
                    add_slot(i, k)
                    make_hot(i + 1, k, l_w, 0, True)
            for k in range(RING):
                add_slot(SLOTS // RING - 1, k)
            dve.wait_ge(slot_added, SLOTS)
            v.sem_inc(agg_ready, 1)
            link(v.tensor_scalar(count[:], agg[:, :, EMBC:EMBP], 1.0, None, ALU.max))
            v.reciprocal(count[:], count[:]).then_inc(inv_ready, 1)

            dve.wait_ge(bias_in, 16)
            for m in range(NT):
                for h in range(2):
                    q = V_DEC + 2 * m + h
                    cols = slice(h * HALF, (h + 1) * HALF)
                    link(v.tensor_tensor(X[:, m, cols], X[:, m, cols], b_dec[:, cols], ALU.add))
                    dve.wait_ge(v_full, q + 1)
                    last = v.tensor_tensor(X[:, m, cols], X[:, m, cols], v_bank[q % 2][:], ALU.add)
                    last.then_inc(v_read, 1)
                if m >= 1:
                    dve.wait_ge(v_read, V_DEC + 2 * m)
                    ln_stats(m - 1)
            dve.wait_ge(v_read, V_DEC + 2 * NT)
            ln_stats(NT - 1).then_inc(stats_ready, 1)
            normalise(2, T_LN2)
            link(v.tensor_scalar(X[:, NT - 1, :], X[:, NT - 1, :], pad_mask[:, 2:3], None, ALU.mult))

            q = V_ROUTE
            dve.wait_ge(v_full, q + 1)
            scores = v_bank[q % 2][:, 0:NT * 8].rearrange("p (m e) -> p m e", e=8)
            for m in range(NT):
                last = v.tensor_tensor(logits[:, m, 0:E0], scores[:, m, 0:E0], b_route[:], ALU.add)
            link(last)
            v.sem_inc(v_read, 1)
            for m in range(NT):
                last = v.max(top[:, m, :], logits[:, m, :])
            link(last)
            for m in range(NT):
                last = v.max_index(top_at[:, m, :], top[:, m, :], logits[:, m, :])
            link(last)
            link(v.tensor_copy(top_f[:], top_at[:]))
            v.tensor_tensor(gsm[:, 0, :], top[:, :, 1], top[:, :, 0], ALU.subtract).then_inc(exp_in, 1)
            dve.wait_ge(exp_ready, 1)
            link(v.tensor_scalar(gsm[:, 2, :], gsm[:, 1, :], 1.0, None, ALU.add))
            link(v.reciprocal(gsm[:, 3, :], gsm[:, 2, :]))
            link(v.tensor_tensor(gsm[:, 4, :], gsm[:, 3, :], gsm[:, 1, :], ALU.mult))
            for e in range(E0):
                link(v.scalar_tensor_tensor(gsm[:, 5, :], top_f[:, :, 1], float(e), gsm[:, 4, :], ALU.is_equal, ALU.mult))
                link(v.scalar_tensor_tensor(gates[:, :, e], top_f[:, :, 0], float(e), gsm[:, 3, :], ALU.is_equal, ALU.mult))
                link(v.tensor_tensor(gates[:, :, e], gates[:, :, e], gsm[:, 5, :], ALU.add))
            link(v.tensor_scalar(gates[:, NT - 1, :], gates[:, NT - 1, :], pad_mask[:, 1:2], pad_mask[:, 0:1], ALU.mult, ALU.add))
            dve.wait_ge(gelu_b_ready, 1)
            with dve.Fori(0, E0) as e:
                for g, (lo, n) in enumerate(TOKG):
                    for c in range(KH):
                        j = g * KH + c
                        dve.wait_ge(a_read, KH * len(TOKG) * e + A_UP + j + 1)
                        v.tensor_scalar(hT[:, c, lo:lo + n], hT[:, c, lo:lo + n], g_up[:, bass.ds(KH * e + c, 1)], None,
                                        ALU.subtract).then_inc(hidden_ready, 1)
                dve.wait_ge(hidden_ready, 16 * e + 12)
                col = (NT - 1) * P + SUMROW
                for c in range(KH):
                    v.tensor_scalar(hT[:, c, col:col + 1], ones[:, 0:1], g_up[:, bass.ds(KH * e + c, 1)], None,
                                    ALU.mult).then_inc(hidden_ready, 1)
                for m in range(NT):
                    for h in range(2):
                        j = 2 * m + h
                        cols = slice(h * HALF, (h + 1) * HALF)
                        dve.wait_ge(v_full, 2 * NT * e + V_DOWN + j + 1)
                        v.scalar_tensor_tensor(X[:, m:m + 1, cols], v_bank[(V_DOWN + j) % 2][:].rearrange("p (o n) -> p o n", o=1),
                                               gates[:, m, bass.ds(e, 1)], X[:, m:m + 1, cols], ALU.mult, ALU.add).then_inc(v_read, 1)
            dve.wait_ge(v_full, V_CSUM + 2)
            for m in range(NT):
                for h in range(2):
                    cols = slice(h * HALF, (h + 1) * HALF)
                    last = v.tensor_tensor(X[:, m, cols], X[:, m, cols], v_bank[(V_CSUM + h) % 2][:], ALU.add)
                link(last)
                last = ln_stats(m)
            v.sem_inc(v_read, 2)
            last.then_inc(stats_ready, 1)
            normalise(3, T_LN3)

            dve.wait_ge(bias_in, 32)
            for h in range(2):
                for m in range(NT):
                    q = V_ROOT + h * NT + m
                    cols = slice(h * HALF, (h + 1) * HALF)
                    dve.wait_ge(v_full, q + 1)
                    v.tensor_tensor(u_rows[:, m, cols], v_bank[q % 2][:], b_rgcn[:, cols], ALU.add).then_inc(v_read, 1)
            dve.wait_ge(inv_listed, 1)
            for k in range(RING):
                make_hot(0, k, l_inv, SLOTS, False)

            def add_slot2(i, k):
                t = dve.value_load(l_tile[0:1, bass.ds(RING * i + k, 1)], min_val=0, max_val=NT - 1)
                dve.wait_ge(slot_summed, RING * i + (SLOTS + RING + k + 1))
                dve.wait_ge(slot_added, RING * i + (SLOTS + k))
                v.tensor_tensor(u_rows[:, bass.ds(t, 1), :], pairs[(k + 1) % 4][:].rearrange("p (o n) -> p o n", o=1),
                                u_rows[:, bass.ds(t, 1), :], ALU.add).then_inc(slot_added, 1)

            dve.wait_ge(v_read, V_GATE)
            with dve.Fori(0, SLOTS // RING - 1) as i:
                for k in range(RING):
                    add_slot2(i, k)
                    make_hot(i + 1, k, l_inv, SLOTS, False)
            for k in range(RING):
                add_slot2(SLOTS // RING - 1, k)
            dve.wait_ge(slot_added, 2 * SLOTS)
            v.sem_inc(agg_ready, 1)

            dve.wait_ge(gate_bias_in, 16)
            for n in range(2 * NT):
                h, m = divmod(n, NT)
                b = n % 2
                q = V_GATE + n
                cols = slice(h * HALF, (h + 1) * HALF)
                link(v.tensor_scalar(xn_half[:, b, :], X[:, m, cols], mv[:, m, 0:1], rstd[:, m:m + 1], ALU.subtract, ALU.mult))
                dve.wait_ge(tanh_ready, n + 1)
                link(v.tensor_tensor(mixed[:, b, :], mixed[:, b, :], xn_half[:, b, :], ALU.subtract))
                dve.wait_ge(v_full, q + 1)
                v.tensor_tensor(OS[:, b, :], v_bank[q % 2][:], b_gate[:, cols], ALU.add).then_inc(v_read, 1)
                dve.wait_ge(v_read, q + 1)
                link(v.tensor_tensor(mixed[:, b, :], mixed[:, b, :], OS[:, b, :], ALU.mult))
                link(v.tensor_tensor(mixed[:, b, :], mixed[:, b, :], xn_half[:, b, :], ALU.add))
                v.tensor_tensor(X[:, m, cols], X[:, m, cols], mixed[:, b, :], ALU.add).then_inc(mixed_ready, 1)
            dve.wait_ge(mixed_ready, 2 * NT)
            for m in range(NT):
                last = ln_stats(m)
            last.then_inc(stats_ready, 1)
            normalise(4, T_LN4, stored=True)

            q = V_ROUTE2
            link(v.tensor_tensor(b_route2[:, 0, :], b_route2[:, 0, :], b_route2[:, 1, :], ALU.add))
            dve.wait_ge(v_full, q + 1)
            scores = v_bank[q % 2][:, 0:NT * 8].rearrange("p (m e) -> p m e", e=8)
            for m in range(NT):
                last = v.tensor_tensor(logits[:, m, :], scores[:, m, :], b_route2[:, 0, :], ALU.add)
            link(last)
            v.sem_inc(v_read, 1)
            for m in range(NT):
                last = v.max(top[:, m, :], logits[:, m, :])
            link(last)
            for m in range(NT):
                last = v.max_index(top_at[:, m, :], top[:, m, :], logits[:, m, :])
            link(last)
            link(v.tensor_copy(top_f[:], top_at[:]))
            link(v.tensor_tensor(tok_key[:], top_f[:, :, 0], tok_pad[:], ALU.add))
            sort(tok_key[:], E1, NT, tok_hot[:], tok_cum[:], tok_pos[:], v_bank[V_PRE2 % 2], V_PRE2, gsm[:, 0, :])
            slot_groups(slot_exp[:], slot_tmp[:], TSLOTS, E1)
            link(v.tensor_copy(tok_posi[:], tok_pos[:]))
            link(v.tensor_scalar(tok_t[:, 0, :], tok_posi[:], P - 1, None, ALU.bitwise_and))
            link(v.tensor_scalar(tok_t[:, 1, :], tok_posi[:], 7, None, ALU.arith_shift_right))
            v.tensor_copy(tok_lane[:], tok_t[:, 0, :])
            link(v.tensor_copy(tok_slot[:], tok_t[:, 1, :]))
            for t in range(NT):
                v.tensor_scalar(tok_perm_lane[:, t, :], iota_free[:, 0:P], tok_lane[:, t:t + 1], None, ALU.is_equal)
                last = v.tensor_scalar(tok_perm_val[:, t, :], iota_free[:, 0:TSLOTS], tok_slot[:, t:t + 1], tok_id[:, t:t + 1],
                                       ALU.is_equal, ALU.mult)
            last.then_inc(tok_perm_ready, 1)
            dve.wait_ge(v_full, V_LIST2 + 1)
            link(v.tensor_copy(tok_list[:], v_bank[V_LIST2 % 2][:, 0:TSLOTS]))
            v.sem_inc(v_read, 1)
            v.sem_inc(tok_list_ready, 1)
            v.sem_inc(tok_bias_free, 2)

            with dve.Fori(0, TSLOTS // 2) as i:
                for b in range(2):
                    s = 2 * i + b
                    dve.wait_ge(tok_bias_in[b], 32 * i + 32)
                    dve.wait_ge(v_full, 3 * s + V_SLOT + 1)
                    v.tensor_tensor(tok_h[:, b, :], v_bank[(3 * b + V_SLOT) % 2][:], tok_b1[:, b, 0:HID], ALU.add).then_inc(tok_h_ready, 1)
                    dve.wait_ge(tok_h_ready, s + 1)
                    dve.sem_inc(v_read, 1)
                    for h in range(2):
                        n = NT + 2 * NT * REL + 2 * b + h
                        k = n % 4
                        dve.wait_ge(os_out[k], 16 * i + 16 * (n // 4))
                        dve.wait_ge(v_full, 3 * s + V_SLOT + 2 + h)
                        v.tensor_tensor(OS[:, k, :], v_bank[(3 * b + V_SLOT + 1 + h) % 2][:], tok_b2[:, b, h * HALF:(h + 1) * HALF],
                                        ALU.add).then_inc(tok_out_ready, 1)
                        dve.wait_ge(tok_out_ready, 2 * s + h + 1)
                        dve.sem_inc(v_read, 1)
                    dve.sem_inc(tok_bias_free, 1)
            for m in range(NT):
                rows = rows_of(m)
                dve.wait_ge(moe_in[m], 16)
                v.tensor_tensor(X[0:rows, m, :], X[0:rows, m, :], moe_rows[0:rows, m, :], ALU.add).then_inc(out_ready, 1)


def kernel(**inputs):
    import concourse.bacc as bacc
    from concourse.bass_utils import run_bass_kernel_spmd

    x = {k: np.asarray(v) for k, v in inputs.items()}

    def padded(a, shape, fill=0):
        return np.pad(a, [(0, n - m) for n, m in zip(shape, a.shape)], constant_values=fill)

    arrays = {k: np.ascontiguousarray(x[k]) for k in (
        "x", "L0_gnn_bdec", "L0_ffn_w1", "L0_ffn_w2", "L0_ffn_b2", "L0_ffn_wr", "L0_ffn_br", "L1_gnn_weight",
        "L1_gnn_root", "L1_gnn_bias", "L1_gnn_w_gate", "L1_gnn_b_gate", "L1_ffn_gate_b", "L1_ffn_expert_bias",
        "L1_ffn_w1", "L1_ffn_b1", "L1_ffn_w2", "L1_ffn_b2")}
    for name, fill in (("src", 0), ("dst", NPAD), ("edge_type_8", 0), ("edge_weight", 0)):
        arrays[name] = padded(x[name], (P * ET,), fill)
    arrays["encT"] = np.ascontiguousarray(padded(x["L0_gnn_wenc"].T, (D, EMBP)))
    arrays["convlin"] = np.concatenate([padded(x["L0_gnn_conv_weight"], (EMBP, EMBP)),
                                        padded(x["L0_gnn_lin_weight"].T, (EMBP, EMBP))])
    arrays["decT"] = np.ascontiguousarray(padded(x["L0_gnn_wdec"].T, (EMBP, D)))
    arrays["b_enc"] = np.ascontiguousarray(padded(x["L0_gnn_benc"], (EMBP,)).reshape(KE, P).T)
    arrays["b_up"] = np.ascontiguousarray(x["L0_ffn_b1"].reshape(E0 * KH, P).T)
    arrays["gate_wT"] = np.ascontiguousarray(x["L1_ffn_gate_w"].T)

    nc = bacc.Bacc("TRN2", target_bir_lowering=False, num_devices=1)
    aps = {k: nc.dram_tensor(f"in_{k}", v.shape, mybir.dt.from_np(v.dtype), kind="ExternalInput").ap() for k, v in arrays.items()}
    out = nc.dram_tensor("out", (N_NODES, D), F32, kind="ExternalOutput").ap()
    build(nc, aps, out)
    r = run_bass_kernel_spmd(nc, [{f"in_{k}": v for k, v in arrays.items()}], core_ids=[0])
    return r.results[0]["out"]
```

```python
from contextlib import ExitStack

import concourse.bass as bass
import numpy as np
from concourse import mybir

F32 = mybir.dt.float32
F32R = mybir.dt.float32r
BF16 = mybir.dt.bfloat16
I32 = mybir.dt.int32
U32 = mybir.dt.uint32
ALU = mybir.AluOpType
ACT = mybir.ActivationFunctionType
AX = mybir.AxisListType

P = 128
N_NODES = 1250
D = 1024
NT = -(-N_NODES // P)
NPAD = NT * P
LAST = N_NODES - (NT - 1) * P
KD = D // P
HALF = 512
EMB = 500
EMBP = 512
EMBC = EMBP - 8
KE = EMBP // P
N_EDGES = 21250
ET = -(-N_EDGES // P)
RING = 8
BATCH = 4
SLOTS = -(-((N_EDGES + NT * (P - 1)) // P) // RING) * RING
REL = 8
E0 = 4
HID = 512
KH = HID // P
E1 = 8
TSLOTS = -(-((N_NODES + E1 * (P - 1)) // P) // 2) * 2
EPS = 1e-5
RELBITS = 3
ROWSHIFT = 14
NOWHERE = 1.0e6
TOKG = [(0, 512), (512, 512), (1024, 256)]
MOEG = [(0, 4), (4, 3), (7, 3)]
SUMROW = LAST

UNIT_ENC, UNIT_CONVLIN, UNIT_DEC, UNIT_E1 = 0, 1, 2, 3
SPLIT_Y = 2 * E0 * len(MOEG)
SPLIT_ROOT = SPLIT_Y + 2 * REL
SPLIT_GATE = SPLIT_ROOT + 2
SPLIT_TOP = SPLIT_GATE + 2

T_LN1 = 0
T_AGG = T_LN1 + 2 * NT
T_LN2 = T_AGG + NT
T_LN3 = T_LN2 + 2 * NT
T_U = T_LN3 + 2 * NT
T_LN4 = T_U + 2 * NT
T_SLOT = T_LN4 + 2 * NT
A_ENC = 0
A_H2 = A_ENC + KE * len(TOKG)
A_LIN = A_H2 + NT
A_UP = A_LIN + NT
A_Y = A_UP + E0 * KH * len(MOEG)
V_PRE = 0

V_DEC = 1
V_ROUTE = V_DEC + 2 * NT
V_DOWN = V_ROUTE + len(TOKG) + 1
V_CSUM = V_DOWN + E0 * 2 * NT
V_ROOT = V_CSUM + 2
V_GATE0 = V_ROOT + 2 * NT
V_GATE = V_GATE0 + 2 * NT
V_ROUTE2 = V_GATE + 2 * NT
V_PRE2 = V_ROUTE2 + len(TOKG) + 1
V_LIST2 = V_PRE2 + 1
V_SLOT = V_LIST2 + 1
O_Y = NT
O_GATE0 = O_Y + 2 * NT * REL
O_MOE = O_GATE0 + 2 * NT
RAW_Y = 16 * 3 * E0 * len(MOEG)
FREE_Y = 13 * E0 * len(MOEG)


def build(nc, a, out):
    ctx = ExitStack()
    with ctx:
        def sb(name, shape, dt=F32):
            return ctx.enter_context(nc.sbuf_tensor(name, shape, dt))

        def sem(name):
            return ctx.enter_context(nc.semaphore(name))

        def dram(name, shape):
            return nc.dram_tensor(name, shape, F32, kind="Internal").ap()

        h2_dram = dram("h2_rows", (NPAD, EMBP))
        y_dram = dram("y_rows", (NPAD, REL, D))
        inv_dram = dram("inv_count", (NPAD, REL))
        x3_dram = dram("x3_rows", (NPAD, D))
        gate0_dram = dram("gate0_rows", (NPAD, D))
        xn_dram = dram("xn_rows", (NPAD, D))
        moe_dram = dram("moe_rows", (TSLOTS * P, D))

        size = dict(x=NT * D, xt=NT * D, u=NT * D, w=8 * D, room=4 * D, xn=2 * D, os=4 * HALF)
        base = -(-nc.sbuf_base // 32) * 32
        at = {}
        for region, n in size.items():
            at[region] = base
            base += 4 * n
        sb("arena", [P, sum(size.values())])

        def place(name, region, shape, dt=F32, skip=0):
            return nc.alloc_sbuf_tensor_at(name, shape, dt, offset=at[region] + 4 * skip)

        X = place("X", "x", [P, NT, D])
        XT = place("XT", "xt", [P, KD, NPAD])
        U = place("U", "u", [P, NT * D])
        W = place("W", "w", [P, 2, 8 * HALF])
        room = place("room", "room", [P, 4, D])
        rows_h2 = room[:].rearrange("p b (c n) -> p (b c) n", n=EMBP)
        rows_y = W[:].rearrange("p b (c n) -> p (b c) n", n=D)
        XN = place("XN", "xn", [P, 2, D])
        OS = place("OS", "os", [P, 4, HALF])
        xh = place("xh", "xt", [P, KD, NPAD], F32R)
        xl = place("xl", "u", [P, KD, NPAD], F32R)
        wh = place("wh", "w", [P, 8, HALF], F32R)
        wl = place("wl", "w", [P, 8, HALF], F32R, skip=8 * HALF)
        raw = place("raw", "room", [P, 8, HALF])
        score_rows = place("score_rows", "xn", [8, NPAD])
        score_rows2 = place("score_rows2", "u", [8, NPAD])
        hh = place("hh", "xn", [P, KH, HALF], F32R)
        hl = place("hl", "os", [P, KH, HALF], F32R)
        h_raw = place("h_raw", "os", [P, KH, HALF])
        gate_h = [place(f"gate_h{h}", r, [P, 8, HALF], F32R) for h, r in enumerate(("xt", "u"))]
        gate_l = [place(f"gate_l{h}", r, [P, 8, HALF], F32R, skip=8 * HALF) for h, r in enumerate(("xt", "u"))]
        raw1 = [place(f"raw1_{h}", r, [P, 4, HALF], skip=16 * HALF) for h, r in enumerate(("xt", "u"))]
        uh = place("uh", "w", [P, 2, KD, P], F32R)
        ul = place("ul", "w", [P, 2, KD, P], F32R, skip=2 * D)
        x3_tile = place("x3_tile", "w", [P, 2, D], skip=4 * D)
        gate0_tile = place("gate0_tile", "w", [P, 2, D], skip=6 * D)
        u_rows = X
        hT = U[:, 0:KE * NPAD].rearrange("p (c n) -> p c n", c=KE)
        agg = U[:, KE * NPAD:].rearrange("p (m n) -> p m n", m=NT)
        lane = U[:, KE * NPAD:]
        used = [0]

        def scratch(n):
            used[0] += n
            assert used[0] <= KE * NPAD
            return lane[:, used[0] - n:used[0]]

        e_dst = scratch(ET).bitcast(I32)
        e_src = scratch(ET).bitcast(I32)
        e_typ = scratch(ET).bitcast(I32)
        e_w = scratch(ET)
        e_t0 = scratch(ET).bitcast(I32)
        e_t1 = scratch(ET).bitcast(I32)
        e_key = scratch(ET)
        e_hot = scratch(NT * ET)
        e_cum = scratch(NT * ET)
        e_pos = scratch(ET)
        e_lane = scratch(ET)
        e_slot = scratch(ET)
        e_pack = e_key
        perm_lane = room[:, :, 0:P]
        perm_val = room[:, :, P:P + 2 * SLOTS]

        iota_free = sb("iota_free", [P, SLOTS])
        iota_part = sb("iota_part", [P, 1])
        ident = sb("ident", [P, P])
        before = sb("before", [P, P])
        ones = sb("ones", [P, P])
        sel_sum = sb("sel_sum", [P, P])
        pad_mask = sb("pad_mask", [P, 3])
        eps = sb("eps", [P, 1])

        l_pack = sb("l_pack", [P, SLOTS], I32)
        l_w = sb("l_w", [P, SLOTS])
        l_src = sb("l_src", [P, SLOTS], I32)
        l_row8 = sb("l_row8", [P, SLOTS], I32)
        l_rel = sb("l_rel", [P, SLOTS])
        l_row = sb("l_row", [P, SLOTS])
        l_tile = sb("l_tile", [P, SLOTS], I32)
        l_inv_at = sb("l_inv_at", [P, SLOTS], I32)
        l_inv = sb("l_inv", [P, SLOTS])
        l_tmp = sb("l_tmp", [P, SLOTS])
        at_ring = sb("at_ring", [P, 2, RING], I32)
        inv_ring = sb("inv_ring", [P, RING])
        hot = XN[:, 0, :].rearrange("p (c n) -> p c n", n=P)
        hot1 = sb("hot1", [P, RING, P], BF16)
        hotr = sb("hotr", [P, RING, REL], BF16)
        count = sb("count", [P, NT, REL])

        pre = sb("pre", [P, 8, NT])
        prei = sb("prei", [P, 2, NT], I32)
        stats = sb("stats", [P, 2, 2, 6])
        mv = sb("mv", [P, NT, 2])
        std = sb("std", [P, NT])
        rstd = sb("rstd", [P, NT])

        b_enc = sb("b_enc", [P, KE])
        b_up = sb("b_up", [P, E0 * KH])
        g_up = sb("g_up", [P, E0 * KH])
        g_up2 = sb("g_up2", [P, E0 * KH])
        b2_rows = sb("b2_rows", [E0, D])
        w_route = sb("w_route", [P, KD, E0])
        route_h = sb("route_h", [P, KD, E0], F32R)
        route_l = sb("route_l", [P, KD, E0], F32R)
        b_route = sb("b_route", [P, E0])
        w_route2 = sb("w_route2", [P, KD, E1])
        b_route2 = sb("b_route2", [P, 2, E1])
        logits = sb("logits", [P, NT, 8])
        top = sb("top", [P, NT, 8])
        top_at = sb("top_at", [P, NT, 8], U32)
        top_f = sb("top_f", [P, NT, 8])
        gsm = sb("gsm", [P, 6, NT])
        gates = sb("gates", [P, NT, E0])
        tok_hot = sb("tok_hot", [P, E1 * NT])
        tok_cum = sb("tok_cum", [P, E1 * NT])
        tok_key = sb("tok_key", [P, NT])
        tok_id = sb("tok_id", [P, NT])
        tok_pad = sb("tok_pad", [P, NT])
        tok_pos = sb("tok_pos", [P, NT])
        tok_posi = sb("tok_posi", [P, NT], I32)
        tok_t = sb("tok_t", [P, 2, NT], I32)
        tok_lane = sb("tok_lane", [P, NT])
        tok_slot = sb("tok_slot", [P, NT])
        tok_list = sb("tok_list", [P, TSLOTS], I32)
        slot_exp = sb("slot_exp", [P, TSLOTS], I32)
        slot_tmp = sb("slot_tmp", [P, TSLOTS])

        b_dec = place("b_dec", "os", [P, D])[:]
        b_rgcn = XN[:, 1, :]
        b_gate = XN[:, 0, :]
        mixed = room[:, 0:2, :]
        xn_tile = room[:, 2:4, :]
        tok_perm_lane = room[:, 0:2, :].rearrange("p b (c n) -> p (b c) n", n=P)
        tok_perm_val = room[:, 2, 0:NT * TSLOTS].rearrange("p (t s) -> p t s", t=NT)
        tok_rows = U[:, 0:2 * D].rearrange("p (b n) -> p b n", b=2)
        tok_xT = U[:, 2 * D:4 * D].rearrange("p (b k n) -> p b k n", b=2, k=KD)
        tok_h = U[:, 4 * D:5 * D].rearrange("p (b n) -> p b n", b=2)
        tok_hT = U[:, 5 * D:6 * D].rearrange("p (b k n) -> p b k n", b=2, k=KH)
        tok_b1 = U[:, 6 * D:7 * D].rearrange("p (b n) -> p b n", b=2)
        tok_b2 = U[:, 7 * D:9 * D].rearrange("p (b n) -> p b n", b=2)
        moe_rows = XT[:].rearrange("p k n -> p (k n)").rearrange("p (m n) -> p m n", m=NT)

        pairs = [ctx.enter_context(nc.psum_tensor(f"pair{i}", [P, D], F32)) for i in range(4)]
        banks = [pairs[i // 2][:, (i % 2) * HALF:(i % 2 + 1) * HALF] for i in range(8)]
        a_bank, v_bank, t_bank = banks[0:2], banks[2:4], banks[4:6]
        sum_bank = [banks[2], banks[3], banks[6], banks[7]]
        list_bank = banks[6]

        def sems(n, *names):
            return [[sem(f"{x}{i}") for i in range(n)] for x in names]

        edges_in, consts_in, bias_in, pad_zero = map(sem, ("edges_in", "consts_in", "bias_in", "pad_zero"))
        (x_in,) = sems(3, "x_in")
        w_in, xn_stored, tok_rows_in, tok_bias_in = sems(2, "w_in", "xn_stored", "tok_rows_in", "tok_bias_in")
        (os_out,) = sems(4, "os_out")
        (rows_in,) = sems(RING, "rows_in")
        (moe_in,) = sems(NT, "moe_in")
        room_zero = sem("room_zero")
        iota_done, consts_ready = sem("iota_done"), sem("consts_ready")
        stats_ready, std_ready, xn_ready = sem("stats_ready"), sem("std_ready"), sem("xn_ready")
        t_full, t_read = sem("t_full"), sem("t_read")
        a_full, a_read = sem("a_full"), sem("a_read")
        v_full, v_read = sem("v_full"), sem("v_read")
        dve_step = sem("dve_step")
        counts_ready = sem("counts_ready")
        perm_ready, perm_done = sem("perm_ready"), sem("perm_done")
        list_ready = sem("list_ready")
        at_ready, issued = sem("at_ready"), sem("issued")
        hot1_ready = sem("hot1_ready")
        hot_ready, slot_added = sem("hot_ready"), sem("slot_added")
        slot_summed = sem("slot_summed")
        inv_ready, inv_stored = sem("inv_ready"), sem("inv_stored")
        inv_in, inv_kept, inv_listed = sem("inv_in"), sem("inv_kept"), sem("inv_listed")
        agg_ready, agg_t_ready = sem("agg_ready"), sem("agg_t_ready")
        gelu_b_ready, hidden_ready = sem("gelu_b_ready"), sem("hidden_ready")
        sum_col_ready, hidden_h_ready = sem("sum_col_ready"), sem("hidden_h_ready")
        exp_in, exp_ready = sem("exp_in"), sem("exp_ready")
        act_turn = sem("act_turn")
        x3_stored = sem("x3_stored")
        route_parts_ready = sem("route_parts_ready")
        xh_ready = sem("xh_ready")
        raw_in, raw1_in = sem("raw_in"), sem("raw1_in")
        w_free = sem("w_free")
        wh_ready, wl_ready = sem("wh_ready"), sem("wl_ready")
        gate_h_ready, gate_l_ready = sem("gate_h_ready"), sem("gate_l_ready")
        uh_ready = sem("uh_ready")
        (tiles_in,) = sems(2, "tiles_in")
        tanh_ready, mixed_ready = sem("tanh_ready"), sem("mixed_ready")
        tok_perm_ready, tok_list_ready = sem("tok_perm_ready"), sem("tok_list_ready")
        tok_bias_free = sem("tok_bias_free")
        tok_h_ready, tok_out_ready = sem("tok_h_ready"), sem("tok_out_ready")
        out_ready, out_done = sem("out_ready"), sem("out_done")
        block = ctx.enter_context(nc.Block())

        def rows_of(m):
            return P if m < NT - 1 else LAST

        def os_uses(k, n):
            return (n - k + 3) // 4

        @block.sync
        def _(sp):
            for dst, src in ((e_dst, a["dst"]), (e_src, a["src"]), (e_typ, a["edge_type_8"]), (e_w, a["edge_weight"])):
                sp.dma_start(dst, src.rearrange("(p t) -> p t", t=ET)).then_inc(edges_in, 16)
            tiles = a["x"][0:(NT - 1) * P, :].rearrange("(m p) d -> p m d", p=P)
            for i in range(2):
                lo, hi = (0, 4) if i == 0 else (4, NT - 1)
                sp.dma_start(X[:, lo:hi, :], tiles[:, lo:hi, :]).then_inc(x_in[i], 16)
            sp.wait_ge(pad_zero, 1)
            sp.dma_start(X[0:LAST, NT - 1, :], a["x"][(NT - 1) * P:N_NODES, :]).then_inc(x_in[2], 16)

            def unit(u):
                return W[:, u % 2, :].rearrange("p (k n) -> p k n", k=8), w_in[u % 2]

            def wide(ap):
                return ap.rearrange("(k p) n -> p k n", p=P)

            w0, s0 = unit(UNIT_ENC)
            sp.dma_start(w0, wide(a["encT"])).then_inc(s0, 16)
            w1, s1 = unit(UNIT_CONVLIN)
            sp.dma_start(w1, wide(a["convlin"])).then_inc(s1, 16)
            for dst, src in (
                (b_enc[:], a["b_enc"]), (b_up[:], a["b_up"]), (b2_rows[:], a["L0_ffn_b2"]),
                (w_route[:], wide(a["L0_ffn_wr"])), (w_route2[:], wide(a["gate_wT"])),
                (b_route[:], a["L0_ffn_br"].partition_broadcast(P)),
                (b_route2[:, 0, :], a["L1_ffn_gate_b"].partition_broadcast(P)),
                (b_route2[:, 1, :], a["L1_ffn_expert_bias"].partition_broadcast(P)),
            ):
                sp.dma_start(dst, src).then_inc(consts_in, 16)
            sp.wait_ge(a_full, A_H2)
            dec = W[:, UNIT_DEC % 2, :].rearrange("p (k n) -> p k n", k=KE)
            sp.dma_start(dec, wide(a["decT"])).then_inc(w_in[UNIT_DEC % 2], 16)
            for k in range(4):
                sp.wait_ge(os_out[k], 16 * os_uses(k, NT))
            sp.dma_start(b_dec, a["L0_gnn_bdec"].partition_broadcast(P)).then_inc(bias_in, 16)
            sp.wait_ge(slot_summed, RING + SLOTS)
            with sp.Fori(0, E0) as e:
                for g in range(len(MOEG)):
                    i = len(MOEG) * e + g
                    sp.wait_ge(wl_ready, 16 * i + 1)
                    src = a["L0_ffn_w1"][bass.ds(e, 1), :, :].rearrange("e (k p) n -> p (e k) n", p=P)
                    sp.dma_start(raw[:], src).then_inc(raw_in, 16)
                    sp.wait_ge(wl_ready, 16 * i + 9)
                    for h in range(2):
                        src = a["L0_ffn_w2"][bass.ds(e, 1), :, h * HALF:(h + 1) * HALF].rearrange("e (k p) n -> p (e k) n", p=P)
                        sp.dma_start(raw[:, h * KH:(h + 1) * KH, :], src).then_inc(raw_in, 16)

            def relation(r, h):
                src = a["L1_gnn_weight"][bass.ds(r, 1), :, h * HALF:(h + 1) * HALF]
                sp.dma_start(raw[:], src.rearrange("r (k p) n -> p (r k) n", p=P)).then_inc(raw_in, 16)

            sp.wait_ge(wl_ready, 8 * SPLIT_Y + 1)
            relation(0, 0)
            sp.wait_ge(stats_ready, 3)
            sp.dma_start(x3_dram.rearrange("(m p) d -> p m d", p=P), X[:]).then_inc(x3_stored, 16)
            sp.wait_ge(wl_ready, 8 * SPLIT_Y + 9)
            relation(0, 1)
            with sp.Fori(1, REL) as r:
                for h in range(2):
                    sp.wait_ge(wl_ready, 16 * r + (8 * SPLIT_Y + 8 * h + 1))
                    relation(r, h)
            sp.wait_ge(t_read, T_LN3 + 2 * NT)
            sp.dma_start(b_rgcn, a["L1_gnn_bias"].partition_broadcast(P)).then_inc(bias_in, 16)
            sp.dma_start(b_gate, a["L1_gnn_b_gate"].partition_broadcast(P)).then_inc(bias_in, 16)
            root = [a["L1_gnn_root"][:, h * HALF:(h + 1) * HALF] for h in range(2)]
            bottom = [a["L1_gnn_w_gate"][D:2 * D, h * HALF:(h + 1) * HALF] for h in range(2)]
            top = [a["L1_gnn_w_gate"][0:D, h * HALF:(h + 1) * HALF] for h in range(2)]
            for u, src in zip(range(SPLIT_ROOT, SPLIT_TOP + 1), root + bottom + top):
                sp.wait_ge(wl_ready, 8 * u + 1)
                sp.dma_start(raw[:], wide(src)).then_inc(raw_in, 16)
            sp.wait_ge(v_full, V_GATE)
            for j in range(2):
                sp.dma_start(raw1[j][:], wide(top[1][4 * j * P:4 * (j + 1) * P, :])).then_inc(raw1_in, 16)
            sp.wait_ge(slot_summed, RING + 2 * SLOTS)
            for k in range(4):
                sp.wait_ge(os_out[k], 16 * os_uses(k, O_MOE))
            for m in range(NT):
                if m >= 2:
                    sp.wait_ge(mixed_ready, m - 1)
                sp.dma_start(x3_tile[:, m % 2, :], x3_dram[m * P:(m + 1) * P, :]).then_inc(tiles_in[m % 2], 16)
                sp.dma_start(gate0_tile[:, m % 2, :], gate0_dram[m * P:(m + 1) * P, :]).then_inc(tiles_in[m % 2], 16)
            sp.wait_ge(tok_list_ready, 1)
            with sp.Fori(0, TSLOTS // 2) as i:
                for b in range(2):
                    e = sp.value_load(slot_exp[0:1, bass.ds(2 * i + b, 1)], min_val=0, max_val=E1 - 1)
                    u = UNIT_E1 + 2 * b
                    sp.wait_ge(v_full, 3 * (2 * i + b) + V_SLOT - 2)
                    w0, s0 = unit(u)
                    src = a["L1_ffn_w1"][bass.ds(e, 1), :, :].rearrange("e (k p) n -> p (e k) n", p=P)
                    sp.dma_start(w0, src).then_inc(s0, 16)
                    sp.wait_ge(tok_bias_free, 2 * i + b + 1)
                    sp.dma_start(tok_b1[:, b, :], a["L1_ffn_b1"][bass.ds(e, 1), :].rearrange("e n -> (e n)").partition_broadcast(P)).then_inc(tok_bias_in[b], 16)
                    sp.dma_start(tok_b2[:, b, :], a["L1_ffn_b2"][bass.ds(e, 1), :].rearrange("e n -> (e n)").partition_broadcast(P)).then_inc(tok_bias_in[b], 16)
                    sp.wait_ge(v_full, 3 * (2 * i + b) + V_SLOT)
                    w1 = W[:, (u + 1) % 2, :].rearrange("p (k n) -> p k n", k=KH)
                    src = a["L1_ffn_w2"][bass.ds(e, 1), :, :].rearrange("e (k p) n -> p (e k) n", p=P)
                    sp.dma_start(w1, src).then_inc(w_in[(u + 1) % 2], 16)
            for m in range(NT):
                sp.wait_ge(out_ready, m + 1)
                sp.dma_start(out[m * P:m * P + rows_of(m), :], X[0:rows_of(m), m, :]).then_inc(out_done, 16)
            sp.wait_ge(out_done, 16 * NT)

        @block.gpsimd
        def _(pool):
            pool.memset(X[96:P, NT - 1, :], 0.0).then_inc(pad_zero, 1)
            pool.wait_ge(pad_zero, 1)
            pool.iota(iota_free[:], [[1, SLOTS]], base=0, channel_multiplier=0,
                      allow_small_or_imprecise_dtypes=True).then_inc(iota_done, 1)
            pool.wait_ge(iota_done, 1)
            pool.iota(iota_part[:], [[0, 1]], base=0, channel_multiplier=1,
                      allow_small_or_imprecise_dtypes=True).then_inc(iota_done, 1)
            pool.wait_ge(iota_done, 2)
            pool.iota(tok_id[:], [[P, NT]], base=0, channel_multiplier=1,
                      allow_small_or_imprecise_dtypes=True).then_inc(iota_done, 1)
            pool.wait_ge(iota_done, 3)
            pool.memset(ident[:], 0.0).then_inc(iota_done, 1)
            pool.wait_ge(iota_done, 4)
            pool.affine_select(out=ident[:], in_=ident[:], compare_op=ALU.not_equal, fill=1.0, base=0,
                               pattern=[[-1, P]], channel_multiplier=1).then_inc(iota_done, 1)
            pool.memset(room[:], 0.0).then_inc(room_zero, 1)

            def gather_slots(table, at_list, rows, done, rounds_done):
                with pool.Fori(0, SLOTS // (2 * RING)) as i:
                    for half in range(2):
                        pool.tensor_copy(at_ring[:, half, :], at_list[:, bass.ds(2 * RING * i + half * RING, RING)]).then_inc(at_ready, 1)
                        for k in range(RING):
                            if k % BATCH == 0:
                                pool.wait_ge(slot_summed, done + 2 * RING * i + half * RING + k + BATCH)
                                pool.sem_inc(issued, 1)
                            if k == 0:
                                pool.wait_ge(at_ready, rounds_done + 2 * i + half + 1)
                                pool.sem_inc(issued, 1)
                            pool.indirect_dma_start(rows(k), None, table,
                                                    bass.IndirectOffsetOnAxis(ap=at_ring[:, half, k:k + 1], axis=0)
                                                    ).then_inc(rows_in[k], 16)

            pool.wait_ge(list_ready, 1)
            for k in range(4):
                pool.wait_ge(os_out[k], 16 * os_uses(k, NT))
            gather_slots(h2_dram, l_src, lambda k: rows_h2[:, k, :], 0, 0)

            pool.wait_ge(inv_stored, 16)
            pool.wait_ge(a_full, A_Y + 1)
            pool.wait_ge(rows_in[RING - 1], 16 * SLOTS // RING)
            inv_rows = inv_dram.rearrange("n (r o) -> (n r) o", o=1)
            with pool.Fori(0, SLOTS // RING) as i:
                pool.tensor_copy(at_ring[:, 0, :], l_inv_at[:, bass.ds(RING * i, RING)]).then_inc(at_ready, 1)
                pool.wait_ge(at_ready, SLOTS // RING + i + 1)
                pool.sem_inc(issued, 1)
                for k in range(RING):
                    pool.indirect_dma_start(inv_ring[:, k:k + 1], None, inv_rows,
                                            bass.IndirectOffsetOnAxis(ap=at_ring[:, 0, k:k + 1], axis=0)
                                            ).then_inc(inv_in, 16)
                pool.wait_ge(inv_in, 16 * RING * (i + 1))
                pool.sem_inc(issued, 1)
                pool.tensor_copy(l_inv[:, bass.ds(RING * i, RING)], inv_ring[:, :]).then_inc(inv_kept, 1)
                pool.wait_ge(inv_kept, i + 1)
                pool.sem_inc(issued, 1)
            pool.sem_inc(inv_listed, 1)

            for k in range(4):
                pool.wait_ge(os_out[k], 16 * os_uses(k, O_GATE0))
            pool.wait_ge(v_full, V_GATE)
            gather_slots(y_dram.rearrange("n r d -> (n r) d"), l_row8, lambda k: rows_y[:, k, :], SLOTS, 2 * SLOTS // RING)

            pool.wait_ge(tok_list_ready, 1)
            for b in range(2):
                pool.wait_ge(xn_stored[b], 16 * NT // 2)
            rounds = 3 * SLOTS // RING
            with pool.Fori(0, TSLOTS // 2) as i:
                for b in range(2):
                    pool.wait_ge(t_full, T_SLOT + 3 * (2 * i + b) - 4)
                    pool.sem_inc(issued, 1)
                    pool.tensor_copy(at_ring[:, 0, b:b + 1], tok_list[:, bass.ds(2 * i + b, 1)]).then_inc(at_ready, 1)
                    pool.wait_ge(at_ready, rounds + 2 * i + b + 1)
                    pool.sem_inc(issued, 1)
                    pool.indirect_dma_start(tok_rows[:, b, :], None, xn_dram,
                                            bass.IndirectOffsetOnAxis(ap=at_ring[:, 0, b:b + 1], axis=0)
                                            ).then_inc(tok_rows_in[b], 16)
            total = O_MOE + 2 * TSLOTS
            for k in range(4):
                pool.wait_ge(os_out[k], 16 * os_uses(k, total))
            for m in range(NT):
                pool.indirect_dma_start(moe_rows[0:rows_of(m), m, :], None, moe_dram,
                                        bass.IndirectOffsetOnAxis(ap=tok_posi[0:rows_of(m), m:m + 1], axis=0)
                                        ).then_inc(moe_in[m], 16)

        @block.tensor
        def _(pe):
            mm = nc.tensor.matmul
            pe.sem_inc(slot_summed, RING)

            def unit(u, wide=8):
                return W[:, u % 2, :].rearrange("p (k n) -> p k n", k=wide)

            def uses(u):
                return u // 2 + 1

            def transpose4(n, blocks):
                pe.wait_ge(t_read, n - 1) if not isinstance(n, int) or n >= 2 else None
                for j, blk in enumerate(blocks):
                    last = nc.tensor.transpose(t_bank[t_slot(n)][:, j * P:(j + 1) * P], blk, ident[:])
                return last.then_inc(t_full, 1)

            def t_slot(n):
                return n % 2

            def transpose_x(base):
                for m in range(NT):
                    pe.wait_ge(xn_ready, (base_ln[base]) * NT + m + 1)
                    for j in range(2):
                        transpose4(base + 2 * m + j, [XN[:, m % 2, (4 * j + q) * P:(4 * j + q + 1) * P] for q in range(4)])

            base_ln = {T_LN1: 0, T_LN2: 1, T_LN3: 2, T_LN4: 3}

            pe.wait_ge(consts_ready, 1)
            pe.wait_ge(counts_ready, 1)
            mm(v_bank[0][:, 0:NT], before[:], pre[:, 1, :], start=True, stop=True)
            mm(v_bank[0][:, 16:16 + NT], ones[:], pre[:, 1, :], start=True, stop=True).then_inc(v_full, 1)
            transpose_x(T_LN1)

            def permute(t, k, first=False, final=False):
                pe.wait_ge(perm_ready, t + 1)
                mm(list_bank[:, 0:2 * SLOTS], perm_lane[:, k, :], perm_val[:, k, :],
                   start=first, stop=final).then_inc(perm_done, 1)

            column = iter(range(ET))

            def next_column():
                t = next(column)
                permute(t, t % 4, first=(t == 0))

            pe.wait_ge(w_in[0], 16)
            w = unit(UNIT_ENC)
            for g, (lo, n) in enumerate(TOKG):
                pe.wait_ge(t_read, T_LN1 + 2 * min(NT, (lo + n) // P))
                for c in range(KE):
                    q = A_ENC + g * KE + c
                    if q >= 2:
                        pe.wait_ge(a_read, q - 1)
                    for k in range(KD):
                        last = mm(a_bank[q % 2][:, 0:n], w[:, k, c * P:(c + 1) * P], XT[:, k, lo:lo + n],
                                  start=(k == 0), stop=(k == KD - 1))
                        if k == KD - 1:
                            last.then_inc(a_full, 1)
                        if q >= A_ENC + 2:
                            next_column()
            last_enc = A_ENC + KE * len(TOKG)

            pe.wait_ge(w_in[1], 16)
            pe.wait_ge(a_read, last_enc)
            w = unit(UNIT_CONVLIN)

            def from_h(base, k0, between=lambda: None):
                for m in range(NT):
                    q = base + m
                    pe.wait_ge(a_read, q - 1)
                    for k in range(KE):
                        last = mm(a_bank[q % 2][:], hT[:, k, m * P:(m + 1) * P], w[:, k0 + k, :],
                                  start=(k == 0), stop=(k == KE - 1))
                        if k == KE - 1:
                            last.then_inc(a_full, 1)
                        between()

            from_h(A_H2, 0, next_column)
            begun = next(column)
            tail = (ET - begun) % 4 or 4
            with pe.Fori(0, (ET - begun - tail) // 4) as i:
                for j in range(4):
                    permute(4 * i + begun + j, (begun + j) % 4)
            for t in range(ET - tail, ET):
                permute(t, t % 4, final=(t == ET - 1))

            from_h(A_LIN, KE)

            def slot_sum(i, k, first=False):
                if not first or k >= 4:
                    pe.wait_ge(slot_added, RING * i + (k - 3))
                pe.wait_ge(hot_ready, RING * i + k + 1)
                pe.wait_ge(rows_in[k], 16 * i + 16)
                mm(sum_bank[k % 4][:, EMBC:EMBP], hot1[:, k, :], hotr[:, k, :], start=True, stop=True)
                mm(sum_bank[k % 4][:, 0:EMBC], hot[:, k, :], rows_h2[:, k, 0:EMBC], start=True, stop=True).then_inc(slot_summed, 1)

            for k in range(RING):
                slot_sum(0, k, first=True)
            with pe.Fori(1, SLOTS // RING) as i:
                for k in range(RING):
                    slot_sum(i, k)

            pe.wait_ge(agg_ready, 1)
            pe.wait_ge(w_in[0], 16 * uses(UNIT_DEC))
            w = unit(UNIT_DEC, KE)
            for m in range(NT + 1):
                if m < NT:
                    transpose4(T_AGG + m, [agg[:, m, c * P:(c + 1) * P] for c in range(KE)])
                if m >= 1:
                    pe.wait_ge(t_read, T_AGG + m)
                    for h in range(2):
                        q = V_DEC + 2 * (m - 1) + h
                        pe.wait_ge(v_read, q - 1)
                        for k in range(KE):
                            last = mm(v_bank[q % 2][:], hT[:, k, (m - 1) * P:m * P], w[:, k, h * HALF:(h + 1) * HALF],
                                      start=(k == 0), stop=(k == KE - 1))
                        last.then_inc(v_full, 1)

            def route(q, products, n, rows):
                for g, (lo, cnt) in enumerate(TOKG):
                    pe.wait_ge(v_read, q + g - 1)
                    for k in range(KD):
                        for i, (weights, xT) in enumerate(products):
                            last = mm(v_bank[(q + g) % 2][0:n, 0:cnt], weights[:, k, :], xT[:, k, lo:lo + cnt],
                                      start=(k + i == 0), stop=(k == KD - 1 and i == len(products) - 1))
                    last.then_inc(v_full, 1)
                pe.wait_ge(v_read, q + len(TOKG))
                for m in range(NT):
                    last = nc.tensor.transpose(v_bank[(q + len(TOKG)) % 2][:, m * 8:m * 8 + n], rows[0:n, m * P:(m + 1) * P], ident[0:n, 0:n])
                last.then_inc(v_full, 1)

            transpose_x(T_LN2)
            pe.wait_ge(t_read, T_LN2 + 2 * NT)
            pe.wait_ge(route_parts_ready, 1)
            route(V_ROUTE, ((route_h, xh), (route_h, xl), (route_l, xh)), E0, score_rows)
            with pe.Fori(0, E0) as e:
                for g, (m0, tiles) in enumerate(MOEG):
                    i = len(MOEG) * e + g
                    cols = slice(m0 * P, (m0 + tiles) * P)
                    for c in range(KH):
                        pe.wait_ge(a_read, KH * i + (A_UP + c - 1))
                        o = a_bank[(A_UP + c) % 2][:, 0:tiles * P]
                        for k in range(KD):
                            if c == 0:
                                pe.wait_ge(wl_ready, 16 * i + (k + 2))
                            part = slice(c * P, (c + 1) * P)
                            mm(o, wh[:, k, part], xh[:, k, cols], start=(k == 0), stop=False)
                            mm(o, wh[:, k, part], xl[:, k, cols], start=False, stop=False)
                            last = mm(o, wl[:, k, part], xh[:, k, cols], start=False, stop=(k == KD - 1))
                            if c == KH - 1 and k < KD - 1:
                                last.then_inc(w_free, 1)
                        last.then_inc(a_full, 1)
                    for m in range(tiles):
                        rows = slice(m * P, (m + 1) * P)
                        for h in range(2):
                            j = 2 * (m0 + m) + h
                            pe.wait_ge(v_read, 2 * NT * e + V_DOWN + j - 1)
                            o = v_bank[(V_DOWN + j) % 2]
                            for k in range(KH):
                                piece = h * KH + k
                                if m == 0:
                                    pe.wait_ge(wl_ready, 16 * i + (8 + piece + 2))
                                    if h == 0:
                                        pe.wait_ge(hidden_ready, KH * i + (k + 1))
                                mm(o, hh[:, k, rows], wh[:, piece, :], start=(k == 0), stop=False)
                                mm(o, hl[:, k, rows], wh[:, piece, :], start=False, stop=False)
                                last = mm(o, hh[:, k, rows], wl[:, piece, :], start=False, stop=(k == KH - 1))
                                if m == tiles - 1 and k < KH - 1:
                                    last.then_inc(w_free, 1)
                            last.then_inc(v_full, 1)
            pe.wait_ge(v_read, V_CSUM)
            for h in range(2):
                cols = slice(h * HALF, (h + 1) * HALF)
                mm(v_bank[(V_CSUM + h) % 2][:], sel_sum[:], X[:, NT - 1, cols], start=True, stop=False)
                mm(v_bank[(V_CSUM + h) % 2][:], ones[0:E0, :], b2_rows[:, cols], start=False, stop=True).then_inc(v_full, 1)

            transpose_x(T_LN3)
            pe.wait_ge(t_read, T_LN3 + 2 * NT)

            def split_unit(u, bank, full, read, base):
                for m in range(NT):
                    cols = slice(m * P, (m + 1) * P)
                    pe.wait_ge(read, base + (m - 1))
                    for k in range(KD):
                        if m == 0:
                            pe.wait_ge(wl_ready, 8 * u + (k + 2))
                        o = bank[m % 2]
                        mm(o, xh[:, k, cols], wh[:, k, :], start=(k == 0), stop=False)
                        mm(o, xl[:, k, cols], wh[:, k, :], start=False, stop=False)
                        last = mm(o, xh[:, k, cols], wl[:, k, :], start=False, stop=(k == KD - 1))
                        if m == NT - 1 and k < KD - 1:
                            last.then_inc(w_free, 1)
                    last.then_inc(full, 1)

            with pe.Fori(0, REL) as r:
                for h in range(2):
                    split_unit(2 * r + (SPLIT_Y + h), [a_bank[(A_Y + j) % 2] for j in range(2)], a_full, a_read, 2 * NT * r + (A_Y + h * NT))
            for j in range(4):
                split_unit(SPLIT_ROOT + j, [v_bank[(V_ROOT + i) % 2] for i in range(2)], v_full, v_read, V_ROOT + j * NT)

            pe.wait_ge(v_read, V_GATE)

            def slot_sum2(i, k, first=False):
                done = SLOTS + RING * i + k
                if not first or k >= 4:
                    pe.wait_ge(slot_added, done - 3)
                pe.wait_ge(hot_ready, done + 1)
                pe.wait_ge(rows_in[k], 16 * i + 16 * (SLOTS // RING) + 16)
                pair = pairs[(k + 1) % 4]
                mm(pair[:, 0:HALF], hot[:, k, :], rows_y[:, k, 0:HALF], start=True, stop=True)
                mm(pair[:, HALF:D], hot[:, k, :], rows_y[:, k, HALF:D], start=True, stop=True).then_inc(slot_summed, 1)

            for k in range(RING):
                slot_sum2(0, k, first=True)
            with pe.Fori(1, SLOTS // RING) as i:
                for k in range(RING):
                    slot_sum2(i, k)

            pe.wait_ge(agg_ready, 2)

            def transpose_u(m):
                for j in range(2):
                    transpose4(T_U + 2 * m + j, [u_rows[:, m, (4 * j + q) * P:(4 * j + q + 1) * P] for q in range(4)])

            transpose_u(0)
            for m in range(NT):
                if m + 1 < NT:
                    transpose_u(m + 1)
                pe.wait_ge(t_read, T_U + 2 * m + 2)
                for h in range(2):
                    q = V_GATE + 2 * m + h
                    pe.wait_ge(v_read, q - 1)
                    for k in range(KD):
                        if m == 0:
                            pe.wait_ge(gate_l_ready, 8 * h + k + 1)
                        o = v_bank[q % 2]
                        mm(o, uh[:, m % 2, k, :], gate_h[h][:, k, :], start=(k == 0), stop=False)
                        mm(o, ul[:, m % 2, k, :], gate_h[h][:, k, :], start=False, stop=False)
                        last = mm(o, uh[:, m % 2, k, :], gate_l[h][:, k, :], start=False, stop=(k == KD - 1))
                    last.then_inc(v_full, 1)

            transpose_x(T_LN4)
            pe.wait_ge(t_read, T_LN4 + 2 * NT)
            pe.wait_ge(consts_in, 16 * 8)
            route(V_ROUTE2, ((w_route2, XT),), E1, score_rows2)
            pe.wait_ge(counts_ready, 2)
            pe.wait_ge(v_read, V_PRE2 - 1)
            b = v_bank[V_PRE2 % 2]
            mm(b[:, 0:E1], before[:], pre[:, 1, 0:E1], start=True, stop=True)
            mm(b[:, 16:16 + E1], ones[:], pre[:, 1, 0:E1], start=True, stop=True).then_inc(v_full, 1)
            pe.wait_ge(tok_perm_ready, 1)
            pe.wait_ge(v_read, V_LIST2 - 1)
            for t in range(NT):
                last = mm(v_bank[V_LIST2 % 2][:, 0:TSLOTS], tok_perm_lane[:, t, :], tok_perm_val[:, t, :],
                          start=(t == 0), stop=(t == NT - 1))
            last.then_inc(v_full, 1)

            def transpose_rows(n, b):
                for j in range(2):
                    pe.wait_ge(t_read, n + j - 1)
                    for q in range(4):
                        last = nc.tensor.transpose(t_bank[(3 * b + T_SLOT + j) % 2][:, q * P:(q + 1) * P],
                                                   tok_rows[:, b, (4 * j + q) * P:(4 * j + q + 1) * P], ident[:])
                    last.then_inc(t_full, 1)

            def tok_slot_step(i, b, final=False):
                s = 2 * i + b
                u = UNIT_E1 + 2 * b
                w = unit(u)
                pe.wait_ge(w_in[u % 2], 32 * i + 16 * uses(u))
                pe.wait_ge(t_read, 3 * s + T_SLOT + 2)
                pe.wait_ge(v_read, 3 * s + V_SLOT - 1)
                for k in range(KD):
                    last = mm(v_bank[(3 * b + V_SLOT) % 2][:], tok_xT[:, b, k, :], w[:, k, :],
                              start=(k == 0), stop=(k == KD - 1))
                last.then_inc(v_full, 1)
                if not final:
                    pe.wait_ge(tok_rows_in[1 - b], 16 * i + 16 * (b + 1))
                    for j in range(2):
                        n = 3 * s + T_SLOT + 2 + j
                        pe.wait_ge(t_read, n - 1)
                        for q in range(4):
                            last = nc.tensor.transpose(t_bank[(3 * b + T_SLOT + 2 + j) % 2][:, q * P:(q + 1) * P],
                                                       tok_rows[:, 1 - b, (4 * j + q) * P:(4 * j + q + 1) * P], ident[:])
                        last.then_inc(t_full, 1)
                skip = 2 if final else 0
                pe.wait_ge(tok_h_ready, s + 1)
                n = 3 * s + T_SLOT + 4 - skip
                pe.wait_ge(t_read, n - 1)
                for q in range(KH):
                    last = nc.tensor.transpose(t_bank[(3 * b + T_SLOT + 4) % 2][:, q * P:(q + 1) * P],
                                               tok_h[:, b, q * P:(q + 1) * P], ident[:])
                last.then_inc(t_full, 1)
                w = unit(u + 1, KH)
                pe.wait_ge(w_in[(u + 1) % 2], 32 * i + 16 * uses(u + 1))
                pe.wait_ge(t_read, n + 1)
                for h in range(2):
                    pe.wait_ge(v_read, 3 * s + V_SLOT + h)
                    for k in range(KH):
                        last = mm(v_bank[(3 * b + V_SLOT + 1 + h) % 2][:], tok_hT[:, b, k, :], w[:, k, h * HALF:(h + 1) * HALF],
                                  start=(k == 0), stop=(k == KH - 1))
                    last.then_inc(v_full, 1)

            pe.wait_ge(tok_rows_in[0], 16)
            transpose_rows(T_SLOT, 0)
            with pe.Fori(0, TSLOTS // 2 - 1) as i:
                for b in range(2):
                    tok_slot_step(i, b)
            tok_slot_step(TSLOTS // 2 - 1, 0)
            tok_slot_step(TSLOTS // 2 - 1, 1, final=True)

        @block.scalar
        def _(act):
            def copy(dst, src, func=ACT.Copy, **kw):
                return nc.scalar.activation(dst, src, func, **kw)

            def take_xT(base):
                for m in range(NT):
                    for j in range(2):
                        n = base + 2 * m + j
                        act.wait_ge(t_full, n + 1)
                        copy(XT[:, 4 * j:4 * j + 4, m * P:(m + 1) * P],
                             t_bank[n % 2][:].rearrange("p (q n) -> p q n", q=4)).then_inc(t_read, 1)

            def roots(n):
                act.wait_ge(stats_ready, n)
                nc.scalar.activation(std[:], mv[:, :, 1], ACT.Sqrt, bias=eps[:]).then_inc(std_ready, 1)

            roots(1)
            take_xT(T_LN1)
            act.wait_ge(consts_in, 16 * 8)
            for g, (lo, n) in enumerate(TOKG):
                for c in range(KE):
                    q = A_ENC + g * KE + c
                    act.wait_ge(a_full, q + 1)
                    nc.scalar.activation(hT[:, c, lo:lo + n], a_bank[q % 2][:, 0:n], ACT.Sigmoid,
                                         bias=b_enc[:, c:c + 1]).then_inc(a_read, 1)
            for m in range(NT):
                q, k = A_H2 + m, m % 4
                act.wait_ge(a_full, q + 1)
                if m >= 4:
                    act.wait_ge(os_out[k], 16 * (m // 4))
                copy(OS[:, k, :], a_bank[q % 2][:]).then_inc(a_read, 1)
                act.wait_ge(a_read, q + 1)
                act.dma_start(h2_dram[m * P:(m + 1) * P, :], OS[:, k, :]).then_inc(os_out[k], 16)
            for m in range(NT):
                q = A_LIN + m
                act.wait_ge(a_full, q + 1)
                if m == 0:
                    act.wait_ge(perm_done, ET)
                copy(agg[:, m, :], a_bank[q % 2][:]).then_inc(a_read, 1)

            with act.Fori(0, SLOTS // RING) as i:
                for k in range(RING):
                    if k % BATCH == 0:
                        act.wait_ge(hot1_ready, (RING // BATCH) * i + (k // BATCH + 1))
                        act.sem_inc(act_turn, 1)
                    copy(hot[:, k, :], hot1[:, k, :], scale=l_w[:, bass.ds(RING * i + k, 1)]).then_inc(hot_ready, 1)

            act.wait_ge(inv_ready, 1)
            act.dma_start(inv_dram.rearrange("(m p) r -> p m r", p=P), count[:]).then_inc(inv_stored, 16)

            for m in range(NT):
                n = T_AGG + m
                act.wait_ge(t_full, n + 1)
                copy(hT[:, :, m * P:(m + 1) * P], t_bank[n % 2][:].rearrange("p (q n) -> p q n", q=4)).then_inc(t_read, 1)

            def take_high(base):
                for n in range(base, base + 2 * NT):
                    m, j = divmod(n - base, 2)
                    act.wait_ge(t_full, n + 1)
                    copy(xh[:, 4 * j:4 * j + 4, m * P:(m + 1) * P],
                         t_bank[n % 2][:].rearrange("p (q n) -> p q n", q=4)).then_inc(xh_ready, 1)

            def piece_h(k):
                copy(wh[:, k, :], raw[:, k, :]).then_inc(wh_ready, 1)

            roots(2)
            take_high(T_LN2)
            nc.scalar.activation(g_up[:], b_up[:], ACT.Gelu).then_inc(gelu_b_ready, 1)
            act.wait_ge(exp_in, 1)
            nc.scalar.activation(gsm[:, 1, :], gsm[:, 0, :], ACT.Exp).then_inc(exp_ready, 1)
            act.wait_ge(v_full, V_ROUTE)
            act.wait_ge(raw_in, 16)
            for k in range(KD):
                piece_h(k)
            with act.Fori(0, E0) as e:
                for g, (m0, tiles) in enumerate(MOEG):
                    i = len(MOEG) * e + g
                    for c in range(KH):
                        if c == KH - 1:
                            act.wait_ge(raw_in, 48 * i + 48)
                            for k in range(KD - 1):
                                act.wait_ge(w_free, 13 * i + (k + 1))
                                piece_h(k)
                        act.wait_ge(a_full, KH * i + (A_UP + c + 1))
                        act.sem_inc(act_turn, 1)
                        nc.scalar.activation(h_raw[:, c, 0:tiles * P], a_bank[(A_UP + c) % 2][:, 0:tiles * P], ACT.Gelu,
                                             bias=b_up[:, bass.ds(KH * e + c, 1)]).then_inc(a_read, 1)
                    piece_h(KD - 1)
                    act.wait_ge(raw_in, 48 * i + 64)
                    for k in range(KD):
                        h, k4 = divmod(k, KH)
                        if k4 < KH - 1:
                            act.wait_ge(w_free, 13 * i + (7 + h * (KH - 1) + k4 + 1))
                        else:
                            act.wait_ge(v_full, 2 * NT * e + (V_DOWN + 2 * (m0 + tiles - 1) + h + 1))
                        piece_h(k)

            roots(3)
            take_high(T_LN3)

            def split_h(u, full, group):
                act.wait_ge(raw_in, 16 * u + (RAW_Y + 16))
                for k in range(KD):
                    if k < KD - 1:
                        act.wait_ge(w_free, 7 * u + (FREE_Y - 7 + k + 1))
                    else:
                        act.wait_ge(full, group)
                    piece_h(k)

            with act.Fori(0, REL) as r:
                for h in range(2):
                    for m in range(NT):
                        if m == NT - 1:
                            split_h(2 * r + (h + 1), a_full, 2 * NT * r + (A_Y + (h + 1) * NT))
                        j = h * NT + m
                        n = O_Y + j
                        k = n % 4
                        act.wait_ge(os_out[k], 16 * (2 * NT // 4) * r + 16 * (n // 4))
                        act.wait_ge(a_full, 2 * NT * r + (A_Y + j + 1))
                        copy(OS[:, k, :], a_bank[(A_Y + j) % 2][:]).then_inc(a_read, 1)
                        act.wait_ge(a_read, 2 * NT * r + (A_Y + j + 1))
                        act.dma_start(y_dram[m * P:(m + 1) * P, bass.ds(r, 1), h * HALF:(h + 1) * HALF],
                                      OS[:, k:k + 1, :]).then_inc(os_out[k], 16)
            for j in range(4):
                for m in range(NT):
                    if m == NT - 1 and j < 3:
                        split_h(SPLIT_ROOT - SPLIT_Y + j + 1, v_full, V_ROOT + (j + 1) * NT)
                    if j >= 2:
                        act.wait_ge(v_read, V_ROOT + j * NT + m + 1)
                        k = (O_GATE0 + (j - 2) * NT + m) % 4
                        act.dma_start(gate0_dram[m * P:(m + 1) * P, (j - 2) * HALF:(j - 1) * HALF], OS[:, k, :]).then_inc(os_out[k], 16)
            act.wait_ge(v_full, V_GATE)
            act.wait_ge(raw_in, RAW_Y + 16 * (SPLIT_TOP - SPLIT_Y + 1))
            for k in range(KD):
                copy(gate_h[0][:, k, :], raw[:, k, :]).then_inc(gate_h_ready, 1)
            act.wait_ge(raw1_in, 32)
            for k in range(KD):
                copy(gate_h[1][:, k, :], raw1[k // 4][:, k % 4, :]).then_inc(gate_h_ready, 1)
            for m in range(NT):
                for j in range(2):
                    q = T_U + 2 * m + j
                    act.wait_ge(t_full, q + 1)
                    if m >= 2:
                        act.wait_ge(v_full, V_GATE + 2 * m - 2)
                    copy(uh[:, m % 2, 4 * j:4 * j + 4, :], t_bank[q % 2][:].rearrange("p (q n) -> p q n", q=4)).then_inc(uh_ready, 1)
                if m == 0:
                    act.wait_ge(gate_l_ready, KD)
                if m >= 2:
                    act.wait_ge(mixed_ready, m - 1)
                nc.scalar.activation(mixed[:, m % 2, :], u_rows[:, m, :], ACT.Tanh).then_inc(tanh_ready, 1)

            roots(4)
            for m in range(NT):
                act.wait_ge(xn_ready, 3 * NT + m + 1)
                act.dma_start(xn_dram[m * P:(m + 1) * P, :], XN[:, m % 2, :]).then_inc(xn_stored[m % 2], 16)
                for j in range(2):
                    n = T_LN4 + 2 * m + j
                    act.wait_ge(t_full, n + 1)
                    copy(XT[:, 4 * j:4 * j + 4, m * P:(m + 1) * P],
                         t_bank[n % 2][:].rearrange("p (q n) -> p q n", q=4)).then_inc(t_read, 1)

            def take(n, parity, dst, func=ACT.Copy):
                act.wait_ge(t_full, n + 1)
                copy(dst, t_bank[parity][:].rearrange("p (q n) -> p q n", q=4), func).then_inc(t_read, 1)

            def slot_out(i, b):
                for h in range(2):
                    n = O_MOE + 2 * b + h
                    k = n % 4
                    act.wait_ge(tok_out_ready, 4 * i + (2 * b + h + 1))
                    act.dma_start(moe_dram.rearrange("(s p) d -> s p d", p=P)[bass.ds(2 * i + b, 1), :, h * HALF:(h + 1) * HALF].rearrange("s p d -> p s d"),
                                  OS[:, k:k + 1, :]).then_inc(os_out[k], 16)

            def tok_slot_step(i, b, final=False):
                s = 2 * i + b
                if not final:
                    for j in range(2):
                        take(3 * s + T_SLOT + 2 + j, (3 * b + T_SLOT + 2 + j) % 2, tok_xT[:, 1 - b, 4 * j:4 * j + 4, :])
                skip = 2 if final else 0
                take(3 * s + T_SLOT + 4 - skip, (3 * b + T_SLOT + 4) % 2, tok_hT[:, b, :, :], ACT.Relu)
                slot_out(i, b)

            for j in range(2):
                take(T_SLOT + j, (T_SLOT + j) % 2, tok_xT[:, 0, 4 * j:4 * j + 4, :])
            with act.Fori(0, TSLOTS // 2 - 1) as i:
                for b in range(2):
                    tok_slot_step(i, b)
            tok_slot_step(TSLOTS // 2 - 1, 0)
            tok_slot_step(TSLOTS // 2 - 1, 1, final=True)

        @block.vector
        def _(dve):
            v = nc.vector
            steps = [0]

            def link(ins):
                steps[0] += 1
                ins.then_inc(dve_step, 1)
                dve.wait_ge(dve_step, steps[0])

            def ln_stats(m):
                for h in range(2):
                    last = v.bn_stats(stats[:, m % 2, h, :], X[:, m, h * HALF:(h + 1) * HALF])
                link(last)
                return v.bn_aggr(mv[:, m, :], stats[:, m % 2, :, :].rearrange("p a b -> p (a b)"))

            def second_part(low, high, n, ready):
                dve.wait_ge(*ready)
                v.tensor_tensor(low, t_bank[n % 2][:].rearrange("p (q n) -> p q n", q=4), high.bitcast(F32),
                                ALU.subtract).then_inc(t_read, 1)

            def x_low(m, base):
                for j in range(2):
                    part = (slice(None), slice(4 * j, 4 * j + 4), slice(m * P, (m + 1) * P))
                    second_part(xl[part], xh[part], base + 2 * m + j, (xh_ready, base + 2 * m + j - T_LN2 + 1))

            def normalise(n, base, stored=False, split=False):
                dve.wait_ge(std_ready, n)
                link(v.reciprocal(rstd[:], std[:]))
                for m in range(NT):
                    if m >= 2:
                        dve.wait_ge(t_full, base + 2 * m - 2)
                        if stored:
                            dve.wait_ge(xn_stored[m % 2], 16 * (m // 2))
                    v.tensor_scalar(XN[:, m % 2, :], X[:, m, :], mv[:, m, 0:1], rstd[:, m:m + 1],
                                    ALU.subtract, ALU.mult).then_inc(xn_ready, 1)
                    if split and m >= 1:
                        x_low(m - 1, base)
                if split:
                    x_low(NT - 1, base)

            def keep_scores(q, n, rows):
                for g, (lo, cnt) in enumerate(TOKG):
                    dve.wait_ge(v_full, q + g + 1)
                    v.tensor_copy(rows[0:n, lo:lo + cnt], v_bank[(q + g) % 2][0:n, 0:cnt]).then_inc(v_read, 1)

            def sort(key, groups, cols, onehot, cum, pos, bank, full, tmp, between=lambda: None):
                gs = slice(0, groups)
                for g in range(groups):
                    last = v.tensor_scalar(onehot[:, g * cols:(g + 1) * cols], key, float(g), None, ALU.is_equal)
                link(last)
                link(v.tensor_tensor_scan(cum, onehot, onehot, 0.0, ALU.add, ALU.max))
                ends = cum.rearrange("p (g t) -> p g t", t=cols)[:, :, cols - 1]
                v.memset(pre[:, 2, 0:1], 0.0)
                v.tensor_copy(pre[:, 2, 1:groups], ends[:, 0:groups - 1])
                link(v.tensor_copy(pre[:, 0, gs], ends))
                v.tensor_tensor(pre[:, 1, gs], pre[:, 0, gs], pre[:, 2, gs], ALU.subtract).then_inc(counts_ready, 1)
                between()
                dve.wait_ge(v_full, full + 1)
                link(v.tensor_scalar(prei[:, 0, gs], bank[:, 16:16 + groups], float(P - 1), None, ALU.add))
                link(v.tensor_scalar(prei[:, 1, gs], prei[:, 0, gs], 7, None, ALU.arith_shift_right))
                link(v.tensor_copy(pre[:, 4, gs], prei[:, 1, gs]))
                link(v.tensor_tensor_scan(pre[:, 5, gs], pre[:, 4, gs], pre[:, 4, gs], 0.0, ALU.add, ALU.max))
                link(v.tensor_tensor(pre[:, 6, gs], pre[:, 5, gs], pre[:, 4, gs], ALU.subtract))
                link(v.scalar_tensor_tensor(pre[:, 7, gs], pre[:, 6, gs], float(P), bank[:, 0:groups], ALU.mult, ALU.add))
                v.sem_inc(v_read, 1)
                link(v.scalar_tensor_tensor(pre[:, 3, gs], pre[:, 7, gs], 1.0, pre[:, 2, gs], ALU.subtract, ALU.subtract))
                for g in range(groups):
                    part = slice(g * cols, (g + 1) * cols)
                    last = v.scalar_tensor_tensor(onehot[:, part], cum[:, part], pre[:, 3, g:g + 1], onehot[:, part], ALU.add, ALU.mult)
                v.tensor_scalar(tmp, key, float(groups), NOWHERE, ALU.is_ge, ALU.mult)
                link(last)
                link(v.tensor_reduce(pos, onehot.rearrange("p (g t) -> p t g", t=cols), AX.X, ALU.add))
                link(v.tensor_tensor(pos, pos, tmp, ALU.add))

            def slot_groups(out_i, tmp, n, groups):
                link(v.tensor_scalar(tmp, iota_free[:, 0:n], pre[:, 5, 0:1], None, ALU.is_ge))
                for g in range(1, groups):
                    link(v.scalar_tensor_tensor(tmp, iota_free[:, 0:n], pre[:, 5, g:g + 1], tmp, ALU.is_ge, ALU.add))
                link(v.tensor_scalar(out_i, tmp, float(groups - 1), None, ALU.min))

            v.sem_inc(wl_ready, 1)
            v.memset(ones[:], 1.0)
            v.memset(eps[:], EPS)
            v.memset(logits[:], -3.0e38)
            dve.wait_ge(iota_done, 5)
            v.tensor_scalar(before[:], iota_free[:, 0:P], iota_part[:, 0:1], None, ALU.is_gt)
            v.tensor_scalar(pad_mask[:, 2:3], iota_part[:], float(SUMROW), None, ALU.is_lt)
            link(v.tensor_scalar(pad_mask[:, 0:1], iota_part[:], float(SUMROW), None, ALU.is_equal))
            v.tensor_scalar(sel_sum[:], ones[:], pad_mask[:, 0:1], None, ALU.mult)
            v.tensor_scalar(tok_pad[:], tok_id[:], float(N_NODES), 100.0, ALU.is_ge, ALU.mult)
            v.tensor_scalar(pad_mask[:, 1:2], pad_mask[:, 0:1], -1.0, 1.0, ALU.mult, ALU.add).then_inc(consts_ready, 1)

            dve.wait_ge(edges_in, 64)
            v.tensor_scalar(e_t1, e_dst, P - 1, None, ALU.bitwise_and)
            link(v.tensor_scalar(e_t0, e_dst, 7, None, ALU.arith_shift_right))
            link(v.tensor_copy(e_key, e_t0))

            def first_ln():
                for m in range(NT):
                    if m in (0, 4, NT - 1):
                        dve.wait_ge(x_in[(0, 4, NT - 1).index(m)], 16)
                    last = ln_stats(m)
                last.then_inc(stats_ready, 1)
                normalise(1, T_LN1)

            sort(e_key, NT, ET, e_hot, e_cum, e_pos, v_bank[0], V_PRE, e_lane, first_ln)
            slot_groups(l_tile[:], l_tmp[:], SLOTS, NT)
            link(v.tensor_copy(e_t0, e_pos))
            link(v.tensor_scalar(e_dst, e_t0, P - 1, None, ALU.bitwise_and))
            link(v.tensor_copy(e_lane, e_dst))
            link(v.tensor_scalar(e_dst, e_t0, 7, None, ALU.arith_shift_right))
            link(v.tensor_copy(e_slot, e_dst))
            link(v.scalar_tensor_tensor(e_pack, e_src, float(REL), e_typ, ALU.mult, ALU.add))
            link(v.tensor_scalar(e_pos, e_t1, 1.0, float(1 << ROWSHIFT), ALU.add, ALU.mult))
            link(v.tensor_tensor(e_pack, e_pack, e_pos, ALU.add))
            dve.wait_ge(room_zero, 1)

            def permute(t, k, first=False):
                if not first:
                    dve.wait_ge(perm_done, t - 3)
                col = (lambda ap: ap[:, t:t + 1]) if isinstance(t, int) else (lambda ap: ap[:, bass.ds(t, 1)])
                v.tensor_scalar(perm_lane[:, k, :], iota_free[:, 0:P], col(e_lane), None, ALU.is_equal)
                v.tensor_scalar(perm_val[:, k, 0:SLOTS], iota_free[:], col(e_slot), col(e_pack), ALU.is_equal, ALU.mult)
                v.tensor_scalar(perm_val[:, k, SLOTS:2 * SLOTS], iota_free[:], col(e_slot), col(e_w), ALU.is_equal,
                                ALU.mult).then_inc(perm_ready, 1)

            head = 4
            tail = (ET - head) % 4
            for t in range(head):
                permute(t, t % 4, first=True)
            with dve.Fori(0, (ET - head - tail) // 4) as i:
                for j in range(4):
                    permute(4 * i + head + j, j)
            for t in range(ET - tail, ET):
                permute(t, t % 4)
            dve.wait_ge(perm_done, ET)
            v.tensor_copy(l_w[:], list_bank[:, SLOTS:2 * SLOTS])
            link(v.tensor_copy(l_pack[:], list_bank[:, 0:SLOTS]))
            link(v.tensor_scalar(l_row8[:], l_pack[:], (1 << ROWSHIFT) - 1, None, ALU.bitwise_and))
            link(v.tensor_scalar(l_src[:], l_row8[:], RELBITS, None, ALU.arith_shift_right))
            link(v.tensor_scalar(l_inv_at[:], l_row8[:], REL - 1, None, ALU.bitwise_and))
            link(v.tensor_copy(l_rel[:], l_inv_at[:]))
            link(v.tensor_scalar(l_inv_at[:], l_pack[:], ROWSHIFT, None, ALU.arith_shift_right))
            link(v.tensor_scalar(l_row[:], l_inv_at[:], 1.0, None, ALU.subtract))
            link(v.tensor_scalar(l_tmp[:], l_row[:], 0.0, None, ALU.max))
            link(v.scalar_tensor_tensor(l_tmp[:], l_tile[:], float(P), l_tmp[:], ALU.mult, ALU.add))
            link(v.scalar_tensor_tensor(l_inv_at[:], l_tmp[:], float(REL), l_rel[:], ALU.mult, ALU.add))
            v.sem_inc(list_ready, 1)

            def make_hots(i, b):
                lo = RING * i + BATCH * b
                col = (lambda ap: ap[:, lo:lo + BATCH]) if isinstance(i, int) else (lambda ap: ap[:, bass.ds(lo, BATCH)])
                ks = slice(BATCH * b, BATCH * (b + 1))

                def wide(ap, n):
                    return ap.unsqueeze(2).broadcast_to([P, BATCH, n])

                def iota(n):
                    return iota_free[:, 0:n].unsqueeze(1).broadcast_to([P, BATCH, n])

                v.tensor_tensor(hotr[:, ks, :], iota(REL), wide(col(l_rel), REL), ALU.is_equal)
                v.tensor_tensor(hot1[:, ks, :], iota(P), wide(col(l_row), P), ALU.is_equal).then_inc(hot1_ready, 1)

            def add_slots(i, b, first=False):
                for k in range(BATCH * b, BATCH * (b + 1)):
                    at = l_tile[0:1, RING * i + k:RING * i + k + 1] if isinstance(i, int) else l_tile[0:1, bass.ds(RING * i + k, 1)]
                    t = dve.value_load(at, min_val=0, max_val=NT - 1)
                    dve.wait_ge(slot_summed, RING * i + (RING + k + 1))
                    if not first or k > 0:
                        dve.wait_ge(slot_added, RING * i + k)
                    v.tensor_tensor(agg[:, bass.ds(t, 1), :], sum_bank[k % 4][:].rearrange("p (o n) -> p o n", o=1),
                                    agg[:, bass.ds(t, 1), :], ALU.add).then_inc(slot_added, 1)

            def make_hot(i, k):
                col = (lambda ap: ap[:, RING * i + k:RING * i + k + 1]) if isinstance(i, int) else (lambda ap: ap[:, bass.ds(RING * i + k, 1)])
                v.tensor_scalar(hot[:, k, :], iota_free[:, 0:P], col(l_row), col(l_inv), ALU.is_equal, ALU.mult).then_inc(hot_ready, 1)

            for b in range(RING // BATCH):
                make_hots(0, b)
            dve.wait_ge(a_read, A_LIN + NT)
            for b in range(RING // BATCH):
                add_slots(0, b, first=True)
                make_hots(1, b)
            with dve.Fori(1, SLOTS // RING - 1) as i:
                for b in range(RING // BATCH):
                    add_slots(i, b)
                    make_hots(i + 1, b)
            for b in range(RING // BATCH):
                add_slots(SLOTS // RING - 1, b)
            dve.wait_ge(slot_added, SLOTS)
            v.sem_inc(agg_ready, 1)
            link(v.tensor_scalar(count[:], agg[:, :, EMBC:EMBP], 1.0, None, ALU.max))
            v.reciprocal(count[:], count[:]).then_inc(inv_ready, 1)

            dve.wait_ge(consts_in, 16 * 8)
            link(v.tensor_copy(route_h[:], w_route[:]))
            v.tensor_tensor(route_l[:], w_route[:], route_h[:].bitcast(F32), ALU.subtract).then_inc(route_parts_ready, 1)

            dve.wait_ge(bias_in, 16)
            for m in range(NT):
                for h in range(2):
                    q = V_DEC + 2 * m + h
                    cols = slice(h * HALF, (h + 1) * HALF)
                    link(v.tensor_tensor(X[:, m, cols], X[:, m, cols], b_dec[:, cols], ALU.add))
                    dve.wait_ge(v_full, q + 1)
                    last = v.tensor_tensor(X[:, m, cols], X[:, m, cols], v_bank[q % 2][:], ALU.add)
                    last.then_inc(v_read, 1)
                if m >= 1:
                    dve.wait_ge(v_read, V_DEC + 2 * m)
                    ln_stats(m - 1)
            dve.wait_ge(v_read, V_DEC + 2 * NT)
            ln_stats(NT - 1).then_inc(stats_ready, 1)
            normalise(2, T_LN2, split=True)
            link(v.tensor_scalar(X[:, NT - 1, :], X[:, NT - 1, :], pad_mask[:, 2:3], None, ALU.mult))

            keep_scores(V_ROUTE, E0, score_rows)
            q = V_ROUTE + len(TOKG)
            dve.wait_ge(v_full, q + 1)
            scores = v_bank[q % 2][:, 0:NT * 8].rearrange("p (m e) -> p m e", e=8)
            for m in range(NT):
                last = v.tensor_tensor(logits[:, m, 0:E0], scores[:, m, 0:E0], b_route[:], ALU.add)
            link(last)
            v.sem_inc(v_read, 1)
            for m in range(NT):
                last = v.max(top[:, m, :], logits[:, m, :])
            link(last)
            for m in range(NT):
                last = v.max_index(top_at[:, m, :], top[:, m, :], logits[:, m, :])
            link(last)
            link(v.tensor_copy(top_f[:], top_at[:]))
            v.tensor_tensor(gsm[:, 0, :], top[:, :, 1], top[:, :, 0], ALU.subtract).then_inc(exp_in, 1)
            dve.wait_ge(exp_ready, 1)
            link(v.tensor_scalar(gsm[:, 2, :], gsm[:, 1, :], 1.0, None, ALU.add))
            link(v.reciprocal(gsm[:, 3, :], gsm[:, 2, :]))
            link(v.tensor_tensor(gsm[:, 4, :], gsm[:, 3, :], gsm[:, 1, :], ALU.mult))
            for e in range(E0):
                link(v.scalar_tensor_tensor(gsm[:, 5, :], top_f[:, :, 1], float(e), gsm[:, 4, :], ALU.is_equal, ALU.mult))
                link(v.scalar_tensor_tensor(gates[:, :, e], top_f[:, :, 0], float(e), gsm[:, 3, :], ALU.is_equal, ALU.mult))
                link(v.tensor_tensor(gates[:, :, e], gates[:, :, e], gsm[:, 5, :], ALU.add))
            link(v.tensor_scalar(gates[:, NT - 1, :], gates[:, NT - 1, :], pad_mask[:, 1:2], pad_mask[:, 0:1], ALU.mult, ALU.add))
            dve.wait_ge(gelu_b_ready, 1)
            link(v.tensor_scalar(g_up2[:], g_up[:], 2.0, None, ALU.mult))

            def piece_l(unit, k):
                dve.wait_ge(wh_ready, 8 * unit + (k + 1))
                v.tensor_tensor(wl[:, k, :], raw[:, k, :], wh[:, k, :].bitcast(F32), ALU.subtract).then_inc(wl_ready, 1)

            for k in range(KD):
                piece_l(0, k)
            with dve.Fori(0, E0) as e:
                for g, (m0, tiles) in enumerate(MOEG):
                    i = len(MOEG) * e + g
                    last_group = g == len(MOEG) - 1
                    for c in range(KH):
                        if c == KH - 1:
                            for k in range(KD - 1):
                                piece_l(2 * i + 1, k)
                        bias = g_up[:, bass.ds(KH * e + c, 1)]
                        h_c = h_raw[:, c, 0:tiles * P]
                        high = hh[:, c, 0:tiles * P]
                        dve.wait_ge(a_read, KH * i + (A_UP + c + 1))
                        if last_group:
                            col = (NT - 1 - m0) * P + SUMROW
                            v.tensor_scalar(h_raw[:, c, col:col + 1], ones[:, 0:1], g_up2[:, bass.ds(KH * e + c, 1)], None,
                                            ALU.mult).then_inc(sum_col_ready, 1)
                            dve.wait_ge(sum_col_ready, KH * e + (c + 1))
                        v.tensor_scalar(high, h_c, bias, None, ALU.subtract).then_inc(hidden_h_ready, 1)
                        dve.wait_ge(hidden_h_ready, KH * i + (c + 1))
                        v.scalar_tensor_tensor(hl[:, c, 0:tiles * P], h_c, bias, high.bitcast(F32), ALU.subtract,
                                               ALU.subtract).then_inc(hidden_ready, 1)
                    piece_l(2 * i + 1, KD - 1)
                    for m in range(m0, m0 + tiles):
                        for h in range(2):
                            j = 2 * m + h
                            cols = slice(h * HALF, (h + 1) * HALF)
                            if m == m0 + tiles - 1:
                                for k in range(KH):
                                    piece_l(2 * i + 2, h * KH + k)
                            dve.wait_ge(v_full, 2 * NT * e + V_DOWN + j + 1)
                            v.scalar_tensor_tensor(X[:, m:m + 1, cols], v_bank[(V_DOWN + j) % 2][:].rearrange("p (o n) -> p o n", o=1),
                                                   gates[:, m, bass.ds(e, 1)], X[:, m:m + 1, cols], ALU.mult, ALU.add).then_inc(v_read, 1)
            dve.wait_ge(v_full, V_CSUM + 2)
            for m in range(NT):
                for h in range(2):
                    cols = slice(h * HALF, (h + 1) * HALF)
                    last = v.tensor_tensor(X[:, m, cols], X[:, m, cols], v_bank[(V_CSUM + h) % 2][:], ALU.add)
                link(last)
                last = ln_stats(m)
            v.sem_inc(v_read, 2)
            last.then_inc(stats_ready, 1)
            normalise(3, T_LN3, split=True)

            def split_l(u):
                for k in range(KD):
                    piece_l(u, k)

            with dve.Fori(0, REL) as r:
                for h in range(2):
                    split_l(2 * r + (SPLIT_Y + h + 1))
            dve.wait_ge(bias_in, 48)
            dve.wait_ge(x3_stored, 16)
            for j in range(4):
                for m in range(NT):
                    if m == NT - 1 and j < 3:
                        split_l(SPLIT_ROOT + j + 1)
                    q = V_ROOT + j * NT + m
                    cols = slice((j % 2) * HALF, (j % 2 + 1) * HALF)
                    if j < 2:
                        dve.wait_ge(v_full, q + 1)
                        v.tensor_tensor(u_rows[:, m, cols], v_bank[q % 2][:], b_rgcn[:, cols], ALU.add).then_inc(v_read, 1)
                    else:
                        n = O_GATE0 + (j - 2) * NT + m
                        dve.wait_ge(os_out[n % 4], 16 * (n // 4))
                        dve.wait_ge(v_full, q + 1)
                        v.tensor_tensor(OS[:, n % 4, :], v_bank[q % 2][:], b_gate[:, cols], ALU.add).then_inc(v_read, 1)
            dve.wait_ge(inv_listed, 1)
            dve.wait_ge(v_read, V_GATE)
            for k in range(RING):
                make_hot(0, k)

            def add_slot2(i, k, first=False):
                t = dve.value_load(l_tile[0:1, k:k + 1] if first else l_tile[0:1, bass.ds(RING * i + k, 1)], min_val=0, max_val=NT - 1)
                dve.wait_ge(slot_summed, RING * i + (SLOTS + RING + k + 1))
                dve.wait_ge(slot_added, RING * i + (SLOTS + k))
                v.tensor_tensor(u_rows[:, bass.ds(t, 1), :], pairs[(k + 1) % 4][:].rearrange("p (o n) -> p o n", o=1),
                                u_rows[:, bass.ds(t, 1), :], ALU.add).then_inc(slot_added, 1)

            with dve.Fori(0, SLOTS // RING - 1) as i:
                for k in range(RING):
                    add_slot2(i, k)
                    make_hot(i + 1, k)
            for k in range(RING):
                add_slot2(SLOTS // RING - 1, k)
            dve.wait_ge(slot_added, 2 * SLOTS)
            v.sem_inc(agg_ready, 1)

            for k in range(2 * KD):
                dve.wait_ge(gate_h_ready, k + 1)
                h, k8 = divmod(k, KD)
                src = raw[:, k8, :] if h == 0 else raw1[k8 // 4][:, k8 % 4, :]
                v.tensor_tensor(gate_l[h][:, k8, :], src, gate_h[h][:, k8, :].bitcast(F32), ALU.subtract).then_inc(gate_l_ready, 1)

            def u_low(m):
                for j in range(2):
                    part = (slice(None), m % 2, slice(4 * j, 4 * j + 4), slice(None))
                    second_part(ul[part], uh[part], T_U + 2 * m + j, (uh_ready, 2 * m + j + 1))

            u_low(0)
            for m in range(NT):
                b = m % 2
                if m + 1 < NT:
                    u_low(m + 1)
                dve.wait_ge(tiles_in[b], 32 * (m // 2) + 32)
                link(v.tensor_scalar(xn_tile[:, b, :], x3_tile[:, b, :], mv[:, m, 0:1], rstd[:, m:m + 1], ALU.subtract, ALU.mult))
                dve.wait_ge(tanh_ready, m + 1)
                link(v.tensor_tensor(mixed[:, b, :], mixed[:, b, :], xn_tile[:, b, :], ALU.subtract))
                for h in range(2):
                    q = V_GATE + 2 * m + h
                    cols = slice(h * HALF, (h + 1) * HALF)
                    dve.wait_ge(v_full, q + 1)
                    v.tensor_tensor(gate0_tile[:, b, cols], gate0_tile[:, b, cols], v_bank[q % 2][:], ALU.add).then_inc(v_read, 1)
                dve.wait_ge(v_read, V_GATE + 2 * m + 2)
                link(v.tensor_tensor(mixed[:, b, :], mixed[:, b, :], gate0_tile[:, b, :], ALU.mult))
                link(v.tensor_tensor(mixed[:, b, :], mixed[:, b, :], xn_tile[:, b, :], ALU.add))
                v.tensor_tensor(X[:, m, :], x3_tile[:, b, :], mixed[:, b, :], ALU.add).then_inc(mixed_ready, 1)
                dve.wait_ge(mixed_ready, m + 1)
                last = ln_stats(m)
            last.then_inc(stats_ready, 1)
            normalise(4, T_LN4, stored=True)

            link(v.tensor_tensor(b_route2[:, 0, :], b_route2[:, 0, :], b_route2[:, 1, :], ALU.add))
            keep_scores(V_ROUTE2, E1, score_rows2)
            q = V_ROUTE2 + len(TOKG)
            dve.wait_ge(v_full, q + 1)
            scores = v_bank[q % 2][:, 0:NT * 8].rearrange("p (m e) -> p m e", e=8)
            for m in range(NT):
                last = v.tensor_tensor(logits[:, m, :], scores[:, m, :], b_route2[:, 0, :], ALU.add)
            link(last)
            v.sem_inc(v_read, 1)
            for m in range(NT):
                last = v.max(top[:, m, :], logits[:, m, :])
            link(last)
            for m in range(NT):
                last = v.max_index(top_at[:, m, :], top[:, m, :], logits[:, m, :])
            link(last)
            link(v.tensor_copy(top_f[:], top_at[:]))
            link(v.tensor_tensor(tok_key[:], top_f[:, :, 0], tok_pad[:], ALU.add))
            sort(tok_key[:], E1, NT, tok_hot[:], tok_cum[:], tok_pos[:], v_bank[V_PRE2 % 2], V_PRE2, gsm[:, 0, :])
            slot_groups(slot_exp[:], slot_tmp[:], TSLOTS, E1)
            link(v.tensor_copy(tok_posi[:], tok_pos[:]))
            link(v.tensor_scalar(tok_t[:, 0, :], tok_posi[:], P - 1, None, ALU.bitwise_and))
            link(v.tensor_scalar(tok_t[:, 1, :], tok_posi[:], 7, None, ALU.arith_shift_right))
            v.tensor_copy(tok_lane[:], tok_t[:, 0, :])
            link(v.tensor_copy(tok_slot[:], tok_t[:, 1, :]))
            for t in range(NT):
                v.tensor_scalar(tok_perm_lane[:, t, :], iota_free[:, 0:P], tok_lane[:, t:t + 1], None, ALU.is_equal)
                last = v.tensor_scalar(tok_perm_val[:, t, :], iota_free[:, 0:TSLOTS], tok_slot[:, t:t + 1], tok_id[:, t:t + 1],
                                       ALU.is_equal, ALU.mult)
            last.then_inc(tok_perm_ready, 1)
            dve.wait_ge(v_full, V_LIST2 + 1)
            link(v.tensor_copy(tok_list[:], v_bank[V_LIST2 % 2][:, 0:TSLOTS]))
            v.sem_inc(v_read, 1)
            v.sem_inc(tok_list_ready, 1)
            v.sem_inc(tok_bias_free, 2)

            with dve.Fori(0, TSLOTS // 2) as i:
                for b in range(2):
                    s = 2 * i + b
                    dve.wait_ge(tok_bias_in[b], 32 * i + 32)
                    dve.wait_ge(v_full, 3 * s + V_SLOT + 1)
                    v.tensor_tensor(tok_h[:, b, :], v_bank[(3 * b + V_SLOT) % 2][:], tok_b1[:, b, 0:HID], ALU.add).then_inc(tok_h_ready, 1)
                    dve.wait_ge(tok_h_ready, s + 1)
                    dve.sem_inc(v_read, 1)
                    for h in range(2):
                        n = O_MOE + 2 * b + h
                        k = n % 4
                        dve.wait_ge(os_out[k], 16 * i + 16 * (n // 4))
                        dve.wait_ge(v_full, 3 * s + V_SLOT + 2 + h)
                        v.tensor_tensor(OS[:, k, :], v_bank[(3 * b + V_SLOT + 1 + h) % 2][:], tok_b2[:, b, h * HALF:(h + 1) * HALF],
                                        ALU.add).then_inc(tok_out_ready, 1)
                        dve.wait_ge(tok_out_ready, 2 * s + h + 1)
                        dve.sem_inc(v_read, 1)
                    dve.sem_inc(tok_bias_free, 1)
            for m in range(NT):
                rows = rows_of(m)
                dve.wait_ge(moe_in[m], 16)
                v.tensor_tensor(X[0:rows, m, :], X[0:rows, m, :], moe_rows[0:rows, m, :], ALU.add).then_inc(out_ready, 1)


def kernel(**inputs):
    import concourse.bacc as bacc
    from concourse.bass_utils import run_bass_kernel_spmd

    x = {k: np.asarray(v) for k, v in inputs.items()}

    def padded(a, shape, fill=0):
        return np.pad(a, [(0, n - m) for n, m in zip(shape, a.shape)], constant_values=fill)

    arrays = {k: np.ascontiguousarray(x[k]) for k in (
        "x", "L0_gnn_bdec", "L0_ffn_w1", "L0_ffn_w2", "L0_ffn_b2", "L0_ffn_wr", "L0_ffn_br", "L1_gnn_weight",
        "L1_gnn_root", "L1_gnn_bias", "L1_gnn_w_gate", "L1_gnn_b_gate", "L1_ffn_gate_b", "L1_ffn_expert_bias",
        "L1_ffn_w1", "L1_ffn_b1", "L1_ffn_w2", "L1_ffn_b2")}
    for name, fill in (("src", 0), ("dst", NPAD), ("edge_type_8", 0), ("edge_weight", 0)):
        arrays[name] = padded(x[name], (P * ET,), fill)
    arrays["encT"] = np.ascontiguousarray(padded(x["L0_gnn_wenc"].T, (D, EMBP)))
    arrays["convlin"] = np.concatenate([padded(x["L0_gnn_conv_weight"], (EMBP, EMBP)),
                                        padded(x["L0_gnn_lin_weight"].T, (EMBP, EMBP))])
    arrays["decT"] = np.ascontiguousarray(padded(x["L0_gnn_wdec"].T, (EMBP, D)))
    arrays["b_enc"] = np.ascontiguousarray(padded(x["L0_gnn_benc"], (EMBP,)).reshape(KE, P).T)
    arrays["b_up"] = np.ascontiguousarray(x["L0_ffn_b1"].reshape(E0 * KH, P).T)
    arrays["gate_wT"] = np.ascontiguousarray(x["L1_ffn_gate_w"].T)

    nc = bacc.Bacc("TRN2", target_bir_lowering=False, num_devices=1)
    aps = {k: nc.dram_tensor(f"in_{k}", v.shape, mybir.dt.from_np(v.dtype), kind="ExternalInput").ap() for k, v in arrays.items()}
    out = nc.dram_tensor("out", (N_NODES, D), F32, kind="ExternalOutput").ap()
    build(nc, aps, out)
    r = run_bass_kernel_spmd(nc, [{f"in_{k}": v for k, v in arrays.items()}], core_ids=[0])
    return r.results[0]["out"]
```
